# Optimizing a Trainium2 kernel written in Bass

```python
import numpy as np
import jax
import jax.numpy as jnp

def _softmax(x, axis=-1):
    return jax.nn.softmax(x, axis=axis)

def _gelu(x):
    return jax.nn.gelu(x, approximate=True)

def _silu(x):
    return jax.nn.silu(x)

def _sigmoid(x):
    return jax.nn.sigmoid(x)

def _layernorm(x, axis=-1, eps=1e-05):
    m = jnp.mean(x, axis=axis, keepdims=True)
    v = jnp.var(x, axis=axis, keepdims=True)
    return (x - m) / jnp.sqrt(v + eps)

def _scatter_add(tgt, idx, src, axis=0):
    return tgt.at[idx].add(src)

def _segment_sum(src, seg, n):
    return jax.ops.segment_sum(src, seg, n)
kernel_name = 'mk_adj_preln_d2_adj_r2_454f95'

def setup_inputs(seed: int=0):
    np.random.seed(seed)
    _w = jnp.asarray

    def _rec_inputs():
        import jax
        import jax.numpy as jnp
        _gk = jax.random.key(seed)
        x = -0.0005207 + 1.001 * jax.random.normal(jax.random.fold_in(_gk, 1), (4096, 128), jnp.float32)
        _a = jax.random.bernoulli(jax.random.fold_in(_gk, 2), 0.000976562, (4096, 4096))
        _a = jnp.logical_or(_a, jnp.swapaxes(_a, -1, -2))
        _a = jnp.logical_or(_a, jnp.eye(4096, dtype=bool))
        adj = _a.astype(jnp.int32)
        return (x, adj)
    x, adj = _rec_inputs()

    def _L0_gnn_setup():
        import jax, jax.numpy as jnp
        import numpy as np
        SIZE_U = 2048
        SIZE_V = 2048
        N = SIZE_U + SIZE_V
        D_IN = 128
        QK_DIM = 128
        V_DIM = 128
        HEADS = 2
        DH = QK_DIM // HEADS
        DV = V_DIM // HEADS
        SCALE = DH ** (-0.5)
        NEG_INF = -9000000000000000.0
        key = jax.random.key(seed)
        ks = jax.random.split(key, 8)
        s = 1.0 / np.sqrt(D_IN)
        x = jax.random.normal(ks[0], (N, D_IN), jnp.float32)
        adj = jax.random.randint(ks[1], (N, N), 0, 2, jnp.int32)
        Wq = jax.random.normal(ks[2], (D_IN, QK_DIM), jnp.float32) * s
        Wk = jax.random.normal(ks[3], (D_IN, QK_DIM), jnp.float32) * s
        Wv = jax.random.normal(ks[4], (D_IN, V_DIM), jnp.float32) * s
        weightr = jax.random.normal(ks[5], (V_DIM, V_DIM), jnp.float32) * s
        weightd = jax.random.normal(ks[6], (V_DIM, V_DIM), jnp.float32) * s
        bias = jnp.zeros((V_DIM,), jnp.float32)
        return {'x': x, 'adj': adj, 'Wq': Wq, 'Wk': Wk, 'Wv': Wv, 'weightr': weightr, 'weightd': weightd, 'bias': bias}
    _L0_gnn_all = _L0_gnn_setup()
    _L0_gnn_in = {k: v for k, v in _L0_gnn_all.items() if k in ('Wq', 'Wk', 'Wv', 'weightr', 'weightd', 'bias')}
    del _L0_gnn_all

    def _L1_gnn_setup():
        import jax, jax.numpy as jnp
        import numpy as np
        N = 4096
        D_IN = 128
        D_OUT = 128
        ALPHA = 0.2
        key = jax.random.key(seed)
        k_x, k_adj, k_w, k_a1, k_a2 = jax.random.split(key, 5)
        xx = jax.random.normal(k_x, (N, D_IN), dtype=jnp.float32)
        adj_hat = jax.random.randint(k_adj, (N, N), 0, 2, dtype=jnp.int32)
        weight = jax.random.normal(k_w, (D_IN, D_OUT), dtype=jnp.float32) * (1.0 / np.sqrt(D_IN))
        weight_a1 = jax.random.normal(k_a1, (D_OUT, 1), dtype=jnp.float32) * (1.0 / np.sqrt(D_OUT))
        weight_a2 = jax.random.normal(k_a2, (D_OUT, 1), dtype=jnp.float32) * (1.0 / np.sqrt(D_OUT))
        return {'xx': xx, 'adj_hat': adj_hat, 'weight': weight, 'weight_a1': weight_a1, 'weight_a2': weight_a2}
    _L1_gnn_all = _L1_gnn_setup()
    _L1_gnn_in = {k: v for k, v in _L1_gnn_all.items() if k in ('weight', 'weight_a1', 'weight_a2')}
    del _L1_gnn_all
    return {'x': x, 'adj': adj, 'L0_gnn_Wq': _L0_gnn_in['Wq'], 'L0_gnn_Wk': _L0_gnn_in['Wk'], 'L0_gnn_Wv': _L0_gnn_in['Wv'], 'L0_gnn_weightr': _L0_gnn_in['weightr'], 'L0_gnn_weightd': _L0_gnn_in['weightd'], 'L0_gnn_bias': _L0_gnn_in['bias'], 'L1_gnn_weight': _L1_gnn_in['weight'], 'L1_gnn_weight_a1': _L1_gnn_in['weight_a1'], 'L1_gnn_weight_a2': _L1_gnn_in['weight_a2']}

def reference(x, adj, L0_gnn_Wq, L0_gnn_Wk, L0_gnn_Wv, L0_gnn_weightr, L0_gnn_weightd, L0_gnn_bias, L1_gnn_weight, L1_gnn_weight_a1, L1_gnn_weight_a2):
    import jax
    import jax.numpy as jnp

    def _L0_gnn_ref(x, adj, Wq, Wk, Wv, weightr, weightd, bias):
        import jax, jax.numpy as jnp
        import numpy as np
        SIZE_U = 2048
        SIZE_V = 2048
        N = SIZE_U + SIZE_V
        D_IN = 128
        QK_DIM = 128
        V_DIM = 128
        HEADS = 2
        DH = QK_DIM // HEADS
        DV = V_DIM // HEADS
        SCALE = DH ** (-0.5)
        NEG_INF = -9000000000000000.0
        q = (x @ Wq).reshape(N, HEADS, DH)
        k = (x @ Wk).reshape(N, HEADS, DH)
        v = (x @ Wv).reshape(N, HEADS, DV)
        scores = jnp.einsum('nhd,mhd->hnm', q * SCALE, k)
        scores = jnp.where(adj[None, :, :] > 0, scores, NEG_INF)
        attn = jax.nn.softmax(scores, axis=-1)
        sat = jnp.einsum('hnm,mhd->nhd', attn, v).reshape(N, V_DIM)
        out = jnp.concatenate([sat[:SIZE_U] @ weightr, sat[SIZE_U:] @ weightd], axis=0)
        out = out + bias
        return jax.nn.leaky_relu(out, negative_slope=0.01)

    def _L1_gnn_ref(xx, adj_hat, weight, weight_a1, weight_a2):
        import jax, jax.numpy as jnp
        import numpy as np
        N = 4096
        D_IN = 128
        D_OUT = 128
        ALPHA = 0.2
        h = jnp.matmul(xx, weight)
        f_1 = jnp.matmul(h, weight_a1)
        f_2 = jnp.matmul(h, weight_a2)
        e = jax.nn.leaky_relu(f_1 + f_2.T, negative_slope=ALPHA)
        masked = jnp.where(adj_hat > 0, e, -jnp.inf)
        attention = jax.nn.softmax(masked, axis=-1)
        h_prime = jnp.matmul(attention, h)
        return h_prime
    h = jnp.maximum(_layernorm(x, axis=-1), 0.0)
    x = x + _L0_gnn_ref(h, adj, L0_gnn_Wq, L0_gnn_Wk, L0_gnn_Wv, L0_gnn_weightr, L0_gnn_weightd, L0_gnn_bias)
    h = jnp.maximum(_layernorm(x, axis=-1), 0.0)
    x = x + _L1_gnn_ref(h, adj, L1_gnn_weight, L1_gnn_weight_a1, L1_gnn_weight_a2)
    return x

_drawn_inputs = setup_inputs


def setup_inputs(seed=0):
    import zlib

    import numpy as np

    out = dict(_drawn_inputs(seed))
    spreads = {'L0_gnn_bias': (0.0, 0.1)}
    factors = {'L1_gnn_weight_a1': 3.012}
    for name, (base, spread) in spreads.items():
        noise = np.random.default_rng([zlib.crc32(name.encode()), seed]).standard_normal(out[name].shape)
        drawn = base * np.exp(spread * noise) if base else spread * noise
        out[name] = jnp.asarray(drawn.astype(out[name].dtype))
    for name, factor in factors.items():
        out[name] = (out[name] * factor).astype(out[name].dtype)
    return out
```

```python
from contextlib import ExitStack

import concourse.bass as bass
from concourse import mybir
from concourse.alu_op_type import AluOpType as ALU

F32 = mybir.dt.float32
F32R = mybir.dt.float32r
BF16 = mybir.dt.bfloat16
I32 = mybir.dt.int32
ACT = mybir.ActivationFunctionType
AX = mybir.AxisListType

P = 128
N = 4096
D = 128
HEADS = 2
DH = D // HEADS
CH = 512
NCH = N // CH
NT = N // P
TPC = CH // P
GROUPS = N // CH
UNITS = TPC * GROUPS
STAGES = 4
EPS = 1e-5
MASKED = -float(2 ** 53)
SCALE = float(DH) ** -0.5
SLOPE0 = 0.01
SLOPE1 = 0.2
LOWEST = -3.0e38

FIRST_UNIT_STEP, LAST_UNIT_STEP = 3, 28
UNIT_STEP = [FIRST_UNIT_STEP + u * (LAST_UNIT_STEP - FIRST_UNIT_STEP + 1) // UNITS for u in range(UNITS)]


def units_at(m):
    return [u for u in range(UNITS) if UNIT_STEP[u] == m]


def need(engine, semaphore, value):
    if not isinstance(value, int) or value > 0:
        engine.wait_ge(semaphore, value)


def over_chunks(body):
    def run(engine):
        body(0, 0)
        with engine.Fori(0, (NCH - 2) // 2) as i:
            body(i * 2 + 1, 1)
            body(i * 2 + 2, 0)
        body(NCH - 1, (NCH - 1) % 2)
    return run


def build(nc, x, adj, wq, wk, wv, wo, bias, w1, a12, out):
    q_dram = nc.dram_tensor("q_scaled", (D, N), F32, kind="Internal").ap()
    x1_dram = nc.dram_tensor("x1", (P, NT, D), F32, kind="Internal").ap()
    mask_dram = nc.dram_tensor("mask", (NCH, P, TPC, N), BF16, kind="Internal").ap()
    with ExitStack() as keep:
        def sb(name, shape, dt, ctx=keep):
            return ctx.enter_context(nc.sbuf_tensor(name, shape, dt))

        shared = dict(
            values=sb("values", [P, NT, D], F32),
            mask=sb("mask_sb", [P, 2, TPC, N], BF16),
            ident=sb("ident", [P, P], F32),
            ident16=sb("ident16", [P, P], BF16),
            ones=sb("ones", [P, P], F32),
            stats=sb("stats", [P, NT, 6], F32),
            moments=sb("moments", [P, NT, 2], F32),
            rstd=sb("rstd", [P, NT], F32),
            std=sb("std", [P, NT], F32),
            newton=sb("newton", [P, NT], F32),
            probs=sb("probs", [P, 2, HEADS, CH], F32),
        )
        with ExitStack() as ctx:
            layer0(nc, ctx, shared, x, adj, wq, wk, wv, wo, bias, q_dram, mask_dram, x1_dram)
        with ExitStack() as ctx:
            layer1(nc, ctx, shared, w1, a12, mask_dram, x1_dram, out)


def norm_stats(nc, dve, T, nodes, chain, stats_done, sqrt_done, var_ready):
    for t in range(NT):
        last = nc.vector.bn_stats(T["stats"][:, t, :], nodes[:, t, :])
    last.then_inc(stats_done, 1)
    dve.wait_ge(stats_done, 1)
    for t in range(NT):
        last = nc.vector.bn_aggr(T["moments"][:, t, :], T["stats"][:, t, :])
    last.then_inc(stats_done, 1)
    dve.wait_ge(stats_done, 2)
    var = T["moments"][:, :, 1]
    nc.vector.tensor_scalar(T["newton"][:], var, EPS, None, ALU.add).then_inc(var_ready, 1)
    dve.wait_ge(sqrt_done, 1)
    rstd, std, newton = T["rstd"][:], T["std"][:], T["newton"][:]
    chain(nc.vector.reciprocal(rstd, std))
    chain(nc.vector.tensor_tensor(std, rstd, rstd, ALU.mult))
    chain(nc.vector.tensor_tensor(std, std, newton, ALU.mult))
    chain(nc.vector.tensor_scalar(std, std, -0.5, 1.5, ALU.mult, ALU.add))
    chain(nc.vector.tensor_tensor(rstd, rstd, std, ALU.mult))


def chained(dve, semaphore):
    count = [0]

    def chain(instruction):
        count[0] += 1
        instruction.then_inc(semaphore, 1)
        dve.wait_ge(semaphore, count[0])
    return chain


def layer0(nc, ctx, T, x, adj, wq, wk, wv, wo, bias, q_dram, mask_dram, x1_dram):
    def sb(name, shape, dt):
        return ctx.enter_context(nc.sbuf_tensor(name, shape, dt))

    def sem(name):
        return ctx.enter_context(nc.semaphore("l0_" + name))

    values, mask, probs = T["values"], T["mask"], T["probs"]
    ident, ident16, ones = T["ident"], T["ident16"], T["ones"]
    spare = mask[:, 1].rearrange("p t m -> p (t m)").bitcast(F32)
    nodes = spare[:, 0:NT * D].rearrange("p (t d) -> p t d", d=D)
    centred = spare[:, NT * D:NT * D + 2 * CH].rearrange("p (b n) -> p b n", b=2)
    ht = spare[:, NT * D + 2 * CH:NT * D + 4 * CH].rearrange("p (b n) -> p b n", b=2)
    k_split = [sb(f"k_split{h}", [P, N], F32R) for h in range(HEADS)]
    k_one = [sb(f"k_one{h}", [DH + 1, N], F32R) for h in range(HEADS)]
    q_high = [sb(f"q_high{h}", [P, 2, CH], F32R) for h in range(HEADS)]
    q_low = [sb(f"q_low{h}", [DH + 1, 2, CH], F32R) for h in range(HEADS)]
    q_raw = sb("q_raw", [P, HEADS, CH], F32)
    sums = sb("sums", [P, HEADS, CH], F32)
    staged = sb("staged", [P, STAGES, CH], I32)
    row_max = sb("row_max", [P, HEADS, TPC, GROUPS], F32)
    pause = sb("pause", [P, 1], F32)
    top = sb("top", [P, HEADS * TPC], F32)
    neg_max = sb("neg_max", [P, HEADS * TPC, DH + 1], F32)
    w_k = sb("w_k", [P, HEADS, 2 * DH], F32)
    w_q = sb("w_q", [P, D], F32)
    w_v = sb("w_v", [P, D], F32)
    w_out = sb("w_out", [P, 2, D], F32)
    bias_all = sb("bias_all", [P, D], F32)
    y = sb("y", [P, CH], F32)
    y_act = sb("y_act", [P, CH], F32)
    attended = sb("attended", [P, CH], F32)
    rden = sb("rden", [P, CH], F32)
    x_rows = sb("x_rows", [P, CH], F32)

    scores = [ctx.enter_context(nc.psum_tensor(f"scores{b}", [P, HEADS, CH], F32)) for b in range(2)]
    rough = ctx.enter_context(nc.psum_tensor("rough", [P, HEADS, CH], F32))
    weighted = ctx.enter_context(nc.psum_tensor("weighted", [P, CH], F32))
    misc = ctx.enter_context(nc.psum_tensor("misc", [P, CH], F32))

    ps_t = [weighted, misc]
    ps_k = [scores[0][:, 0, :], scores[0][:, 1, :]]
    ps_q, ps_v = scores[1][:, 0, :], scores[1][:, 1, :]

    x_loaded, w_loaded, b_loaded = sem("x_loaded"), sem("w_loaded"), sem("b_loaded")
    ident_made, consts = sem("ident"), sem("consts")
    stats_done, var_ready, sqrt_done, norm_chain = sem("stats"), sem("var"), sem("sqrt"), sem("chain")
    centred_ready, turned, ht_ready = sem("centred"), sem("turned"), sem("ht")
    projected, k_high_done, k_done, q_done, v_done = (
        sem("projected"), sem("k_high"), sem("k"), sem("q"), sem("v"))
    q_stored, q_raw_loaded = sem("q_stored"), sem("q_raw")
    q_high_done, q_low_done = sem("q_high"), sem("q_low")
    adj_loaded = [sem(f"adj{s}") for s in range(STAGES)]
    mask_done, mask_stored = sem("mask"), sem("mask_stored")
    rough_done, rough_read = sem("rough"), sem("rough_read")
    max_done, max_turned, max_row = sem("max"), sem("max_turned"), sem("max_row")
    scores_done, exp_done, pv_done = sem("scores"), sem("exp"), sem("pv")
    sum_done = [sem("sum0"), sem("sum1")]
    den_done, epilogue, out_done = sem("den"), sem("epilogue"), sem("out")
    x_rows_loaded, x1_stored = sem("x_rows"), sem("x1_stored")

    x_t = x.rearrange("(c p) d -> p c d", p=P)
    adj_t = adj.rearrange("(c p) m -> c p m", p=P)
    NEPI = 5

    with nc.Block() as block:
        @block.sync
        def _(sp):
            for k in range(NCH):
                sp.dma_start(nodes[:, k * TPC:(k + 1) * TPC, :],
                             x_t[:, k * TPC:(k + 1) * TPC, :]).then_inc(x_loaded, 16)
            for h in range(HEADS):
                for twice in range(2):
                    sp.dma_start(w_k[:, h, twice * DH:(twice + 1) * DH],
                                 wk[:, h * DH:(h + 1) * DH]).then_inc(w_loaded, 16)
            sp.dma_start(w_q[:], wq).then_inc(w_loaded, 16)
            sp.dma_start(w_v[:], wv).then_inc(w_loaded, 16)
            sp.dma_start(w_out[:], wo.rearrange("s d e -> d s e")).then_inc(w_loaded, 16)
            sp.dma_start(bias_all[:], bias.partition_broadcast(P)).then_inc(b_loaded, 16)

            def load_adjacency(c, units=range(UNITS)):
                for u in units:
                    g, j = u // TPC, u % TPC
                    need(sp, mask_done, c * UNITS + (u - STAGES + 1))
                    rows = adj_t[bass.ds(c * TPC + j, 1), :, g * CH:(g + 1) * CH]
                    sp.dma_start(staged[:, u % STAGES, :],
                                 rows.rearrange("o p m -> (o p) m")).then_inc(adj_loaded[u % STAGES], 16)

            def load_q(c):
                need(sp, q_low_done, c * HEADS)
                for h in range(HEADS):
                    for twice in range(2):
                        sp.dma_start(q_raw[twice * DH:(twice + 1) * DH, h, :],
                                     q_dram[h * DH:(h + 1) * DH, bass.ts(c, CH)]).then_inc(q_raw_loaded, 16)

            load_adjacency(0, range(STAGES))
            sp.wait_ge(q_stored, 16 * NCH)
            load_q(0)
            load_adjacency(0, range(STAGES, UNITS))

            def chunk(c, par):
                sp.wait_ge(mask_done, (c + 1) * UNITS)
                sp.dma_start(mask_dram[bass.ds(c, 1)].rearrange("o p t m -> (o p) t m"),
                             mask[:, par]).then_inc(mask_stored, 16)
                if not isinstance(c, int) or c + 1 < NCH:
                    load_q(c + 1)
                    load_adjacency(c + 1)
                if not isinstance(c, int) or c > 0:
                    store_x1(c - 1)
                load_x(c)

            def store_x1(e):
                sp.wait_ge(epilogue, (e + 2) * NEPI)
                sp.dma_start(x1_dram[:, bass.ds(e * TPC, TPC), :],
                             y[:].rearrange("p (t d) -> p t d", t=TPC)).then_inc(x1_stored, 16)

            def load_x(e):
                need(sp, x1_stored, e * 16)
                sp.dma_start(x_rows[:].rearrange("p (t d) -> p t d", t=TPC),
                             x_t[:, bass.ds(e * TPC, TPC), :]).then_inc(x_rows_loaded, 16)
            over_chunks(chunk)(sp)
            store_x1(NCH - 1)
            sp.wait_ge(x1_stored, 16 * NCH)
            sp.wait_ge(mask_stored, 16 * NCH)

        @block.gpsimd
        def _(pool):
            nc.gpsimd.memset(ident[:], 0.0).then_inc(ident_made, 1)
            pool.wait_ge(ident_made, 1)
            nc.gpsimd.affine_select(out=ident[:], in_=ident[:], compare_op=ALU.not_equal, fill=1.0,
                                    base=0, pattern=[[-1, P]], channel_multiplier=1).then_inc(ident_made, 1)
            pool.wait_ge(ident_made, 2)
            nc.gpsimd.tensor_copy(ident16[:], ident[:]).then_inc(consts, 1)
            pool.wait_ge(consts, 5)

            def chunk(c, par):
                for m in range(NT):
                    pool.wait_ge(exp_done, c * NT + (m + 1))
                    if m == 0:
                        need(pool, den_done, c)
                        nc.gpsimd.tensor_tensor(sums[:, 0, :], probs[:, 0, 0, :],
                                                ones[:, 0:1].broadcast_to([P, CH]), ALU.mult).then_inc(sum_done[0], 1)
                    else:
                        pool.wait_ge(sum_done[0], c * NT + m)
                        nc.gpsimd.tensor_tensor(sums[:, 0, :], sums[:, 0, :], probs[:, m % 2, 0, :],
                                                ALU.add).then_inc(sum_done[0], 1)
            over_chunks(chunk)(pool)

        @block.scalar
        def _(act):
            act.wait_ge(var_ready, 1)
            nc.scalar.activation(T["std"][:], T["newton"][:], ACT.Sqrt).then_inc(sqrt_done, 1)
            for k in range(NCH):
                cols = slice(k * CH, (k + 1) * CH)
                act.wait_ge(turned, k + 1)
                need(act, projected, 4 * (k - 1))
                nc.scalar.activation(ht[:, k % 2, :], ps_t[k % 2][:], ACT.Relu).then_inc(ht_ready, 1)
                for h in range(HEADS):
                    act.wait_ge(projected, 4 * k + h + 1)
                    nc.scalar.activation(k_split[h][:, cols], ps_k[h], ACT.Copy).then_inc(k_high_done, 1)
                act.wait_ge(projected, 4 * k + 3)
                need(act, q_stored, 16 * k)
                nc.scalar.activation(y[:], ps_q, ACT.Copy, scale=SCALE).then_inc(q_done, 1)
                act.wait_ge(q_done, k + 1)
                act.dma_start(q_dram[:, cols], y[:]).then_inc(q_stored, 16)

            def round_q(c, par):
                act.wait_ge(q_raw_loaded, (c + 1) * 64)
                for h in range(HEADS):
                    nc.scalar.activation(q_high[h][:, par, :], q_raw[:, h, :],
                                         ACT.Copy).then_inc(q_high_done, 1)

            def max_rows(c, par):
                act.wait_ge(max_turned, c + 1)
                for h in range(HEADS):
                    nc.scalar.activation(q_low[h][DH:DH + 1, par, :], rough[DH:DH + 1, h, :],
                                         ACT.Copy).then_inc(max_row, 1)

            round_q(0, 0)
            max_rows(0, 0)

            def chunk(c, par):
                more = not isinstance(c, int) or c + 1 < NCH
                for m in range(NT):
                    s = c * NT + m
                    act.wait_ge(scores_done, s + 1)
                    need(act, pv_done, s - 1)
                    need(act, sum_done[0], s - 1)
                    need(act, sum_done[1], s - 1)
                    nc.scalar.activation(probs[:, m % 2], scores[m % 2][:], ACT.Exp).then_inc(exp_done, 1)
                    if more and m == 0:
                        round_q(c + 1, 1 - par)
                    if more and m == NT - 2:
                        max_rows(c + 1, 1 - par)
            over_chunks(chunk)(act)

        @block.vector
        def _(dve):
            chain = chained(dve, norm_chain)
            nc.vector.memset(ones[:], 1.0).then_inc(consts, 1)
            for h in range(HEADS):
                nc.vector.memset(k_one[h][DH:DH + 1, :].bitcast(F32), 1.0).then_inc(consts, 1)
            nc.vector.memset(neg_max[:], 0.0).then_inc(consts, 1)
            dve.wait_ge(x_loaded, 16 * NCH)
            norm_stats(nc, dve, T, nodes, chain, stats_done, sqrt_done, var_ready)

            def centre(k):
                need(dve, turned, k - 1)
                for j in range(TPC):
                    t = k * TPC + j
                    last = nc.vector.tensor_scalar(centred[:, k % 2, j * P:(j + 1) * P], nodes[:, t, :],
                                                   T["moments"][:, t, 0:1], T["rstd"][:, t:t + 1],
                                                   ALU.subtract, ALU.mult)
                last.then_inc(centred_ready, 1)

            def convert(c, par, u):
                if u == UNITS:
                    nc.vector.memset(pause[:], 0.0)
                    return
                g, j = u // TPC, u % TPC
                dve.wait_ge(adj_loaded[u % STAGES], (c * GROUPS + (g + 1)) * 16)
                nc.vector.tensor_scalar(mask[:, par, j, g * CH:(g + 1) * CH], staged[:, u % STAGES, :],
                                        0.0, MASKED, ALU.is_le, ALU.mult).then_inc(mask_done, 1)

            def top_of(c, par, u):
                g, j = u // TPC, u % TPC
                dve.wait_ge(mask_done, c * UNITS + (u + 1))
                dve.wait_ge(rough_done, c * UNITS + (u + 1))
                convert(c, par, u + 1)
                for h in range(HEADS):
                    last = nc.vector.tensor_tensor_reduce(
                        out=rough[:, h, :], in0=rough[:, h, :], in1=mask[:, par, j, g * CH:(g + 1) * CH],
                        scale=1.0, scalar=LOWEST, op0=ALU.add, op1=ALU.max,
                        accum_out=row_max[:, h, j, g:g + 1])
                last.then_inc(rough_read, 1)

            def maxima(c):
                dve.wait_ge(rough_read, (c + 1) * UNITS)
                nc.vector.tensor_reduce(top[:], row_max[:].rearrange("p h j g -> p (h j) g"), AX.X,
                                        ALU.max).then_inc(max_done, 1)
                dve.wait_ge(max_done, c * 2 + 1)
                nc.vector.tensor_scalar(neg_max[:, :, DH], top[:], -1.0, None,
                                        ALU.mult).then_inc(max_done, 1)

            def lower_q(c, par):
                for h in range(HEADS):
                    dve.wait_ge(q_high_done, c * HEADS + (h + 1))
                    nc.vector.tensor_tensor(q_low[h][0:DH, par, :], q_raw[0:DH, h, :],
                                            q_high[h][0:DH, par, :].bitcast(F32),
                                            ALU.subtract).then_inc(q_low_done, 1)

            centre(0)
            for k in range(NCH):
                cols = slice(k * CH, (k + 1) * CH)
                if k + 1 < NCH:
                    centre(k + 1)
                for h in range(HEADS):
                    dve.wait_ge(k_high_done, HEADS * k + h + 1)
                    nc.vector.tensor_copy(k_one[h][0:DH, cols], k_split[h][0:DH, cols].bitcast(F32))
                    nc.vector.tensor_tensor(k_split[h][DH:P, cols], ps_k[h][DH:P, :],
                                            k_split[h][DH:P, cols].bitcast(F32),
                                            ALU.subtract).then_inc(k_done, 1)
                dve.wait_ge(projected, 4 * k + 4)
                nc.vector.tensor_copy(values[:, k * TPC:(k + 1) * TPC, :].rearrange("p t d -> p (t d)"),
                                      ps_v).then_inc(v_done, 1)

            dve.wait_ge(consts, 5)
            lower_q(0, 0)
            convert(0, 0, 0)
            for u in range(UNITS):
                top_of(0, 0, u)
            maxima(0)
            nc.vector.memset(y_act[:], 0.0).then_inc(epilogue, NEPI)

            def sum_head1(c, m):
                dve.wait_ge(exp_done, c * NT + (m + 1))
                if m == 0:
                    need(dve, den_done, c)
                    nc.vector.tensor_copy(sums[:, 1, :], probs[:, 0, 1, :]).then_inc(sum_done[1], 1)
                else:
                    dve.wait_ge(sum_done[1], c * NT + m)
                    nc.vector.tensor_tensor(sums[:, 1, :], sums[:, 1, :], probs[:, m % 2, 1, :],
                                            ALU.add).then_inc(sum_done[1], 1)

            def divide(e):
                before = (e + 1) * NEPI
                dve.wait_ge(den_done, e + 1)
                nc.vector.reciprocal(rden[:], misc[:]).then_inc(epilogue, 1)
                dve.wait_ge(epilogue, before + 1)
                nc.vector.tensor_tensor(attended[:], weighted[:], rden[:], ALU.mult).then_inc(epilogue, 1)

            def residual(e):
                before = (e + 1) * NEPI
                dve.wait_ge(x_rows_loaded, (e + 1) * 16)
                dve.wait_ge(out_done, e + 1)
                biases = bias_all[:].rearrange("p (o d) -> p o d", o=1).broadcast_to([P, TPC, D])
                nc.vector.tensor_tensor(y[:].rearrange("p (t d) -> p t d", t=TPC),
                                        misc[:].rearrange("p (t d) -> p t d", t=TPC), biases,
                                        ALU.add).then_inc(epilogue, 1)
                dve.wait_ge(epilogue, before + 3)
                nc.vector.scalar_tensor_tensor(y_act[:], y[:], SLOPE0, y[:], ALU.mult,
                                               ALU.max).then_inc(epilogue, 1)
                dve.wait_ge(epilogue, before + 4)
                nc.vector.tensor_tensor(y[:], x_rows[:], y_act[:], ALU.add).then_inc(epilogue, 1)

            def chunk(c, par):
                first = isinstance(c, int) and c == 0
                more = not isinstance(c, int) or c + 1 < NCH
                for m in range(NT):
                    if m > 0:
                        sum_head1(c, m - 1)
                    if m == 0 and not first:
                        divide(c - 1)
                    if m == 1 and more:
                        need(dve, scores_done, c * NT)
                        lower_q(c + 1, 1 - par)
                    if m == 3 and not first:
                        residual(c - 1)
                    if more:
                        if m == FIRST_UNIT_STEP:
                            need(dve, mask_stored, c * 16)
                            convert(c + 1, 1 - par, 0)
                        for u in units_at(m):
                            top_of(c + 1, 1 - par, u)
                        if m == LAST_UNIT_STEP + 1:
                            maxima(c + 1)
                sum_head1(c, NT - 1)
            over_chunks(chunk)(dve)
            divide(NCH - 1)
            residual(NCH - 1)

        @block.tensor
        def _(pe):
            pe.wait_ge(consts, 5)
            pe.wait_ge(w_loaded, 16 * 7)
            pe.wait_ge(b_loaded, 16)

            def turn(k):
                pe.wait_ge(centred_ready, k + 1)
                need(pe, ht_ready, k - 1)
                for j in range(TPC):
                    cols = slice(j * P, (j + 1) * P)
                    last = nc.tensor.transpose(ps_t[k % 2][:, cols], centred[:, k % 2, cols], ident[:])
                last.then_inc(turned, 1)

            turn(0)
            for k in range(NCH):
                if k + 1 < NCH:
                    turn(k + 1)
                pe.wait_ge(ht_ready, k + 1)
                for h in range(HEADS):
                    need(pe, k_done, HEADS * (k - 1) + h + 1)
                    nc.tensor.matmul(ps_k[h], w_k[:, h, :], ht[:, k % 2, :], start=True,
                                     stop=True).then_inc(projected, 1)
                need(pe, q_done, k)
                nc.tensor.matmul(ps_q, w_q[:], ht[:, k % 2, :], start=True, stop=True).then_inc(projected, 1)
                need(pe, v_done, k)
                for j in range(TPC):
                    cols = slice(j * P, (j + 1) * P)
                    last = nc.tensor.matmul(ps_v[:, cols], ht[:, k % 2, cols], w_v[:], start=True, stop=True)
                last.then_inc(projected, 1)

            def rough_scores(c, par, u):
                g, j = u // TPC, u % TPC
                need(pe, rough_read, c * UNITS + u)
                for h in range(HEADS):
                    last = nc.tensor.matmul(rough[:, h, :], q_high[h][:, par, j * P:(j + 1) * P],
                                            k_split[h][:, g * CH:(g + 1) * CH], start=True, stop=True)
                last.then_inc(rough_done, 1)

            def turn_maxima(c):
                pe.wait_ge(max_done, (c + 1) * 2)
                for h in range(HEADS):
                    for j in range(TPC):
                        last = nc.tensor.matmul(rough[0:DH + 1, h, j * P:(j + 1) * P],
                                                neg_max[:, h * TPC + j, :], ident[:], start=True, stop=True)
                last.then_inc(max_turned, 1)

            pe.wait_ge(k_done, HEADS * NCH)
            pe.wait_ge(q_high_done, HEADS)
            for u in range(UNITS):
                rough_scores(0, 0, u)
            turn_maxima(0)

            def score(c, par, m):
                s = c * NT + m
                keys = slice(m * P, (m + 1) * P)
                bank = scores[m % 2]
                if m == 0:
                    pe.wait_ge(q_high_done, (c + 1) * HEADS)
                need(pe, exp_done, s - 1)
                for h in range(HEADS):
                    nc.tensor.matmul(bank[:, h, :], k_split[h][:, keys], q_high[h][:, par, :],
                                     start=True, stop=False)
                if m == 0:
                    pe.wait_ge(mask_done, (c + 1) * UNITS)
                for j in range(TPC):
                    for h in range(HEADS):
                        nc.tensor.matmul(bank[:, h, j * P:(j + 1) * P], mask[:, par, j, keys], ident16[:],
                                         start=False, stop=False)
                if m == 0:
                    pe.wait_ge(q_low_done, (c + 1) * HEADS)
                    pe.wait_ge(max_row, (c + 1) * HEADS)
                for h in range(HEADS):
                    last = nc.tensor.matmul(bank[:, h, :], k_one[h][:, keys], q_low[h][:, par, :],
                                            start=False, stop=True)
                last.then_inc(scores_done, 1)

            def weigh(c, m):
                pe.wait_ge(exp_done, c * NT + (m + 1))
                for h in range(HEADS):
                    last = nc.tensor.matmul(weighted[h * DH:(h + 1) * DH, :],
                                            values[:, m, h * DH:(h + 1) * DH], probs[:, m % 2, h, :],
                                            start=(m == 0), stop=(m == NT - 1))
                last.then_inc(pv_done, 1)

            def denominators(e):
                pe.wait_ge(sum_done[0], (e + 1) * NT)
                pe.wait_ge(sum_done[1], (e + 1) * NT)
                pe.wait_ge(epilogue, (e + 1) * NEPI)
                for h in range(HEADS):
                    last = nc.tensor.matmul(misc[h * DH:(h + 1) * DH, :], ones[:, 0:DH], sums[:, h, :],
                                            start=True, stop=True)
                last.then_inc(den_done, 1)

            def project(e):
                pe.wait_ge(epilogue, (e + 1) * NEPI + 2)
                side = e // (NCH // 2)
                for j in range(TPC):
                    last = nc.tensor.matmul(misc[:, j * P:(j + 1) * P], attended[:, j * P:(j + 1) * P],
                                            w_out[:, bass.ds(side, 1), :].rearrange("p o d -> p (o d)"),
                                            start=True, stop=True)
                last.then_inc(out_done, 1)

            def chunk(c, par):
                first = isinstance(c, int) and c == 0
                more = not isinstance(c, int) or c + 1 < NCH
                for m in range(NT):
                    score(c, par, m)
                    if more:
                        if m == FIRST_UNIT_STEP:
                            pe.wait_ge(q_high_done, (c + 2) * HEADS)
                        for u in units_at(m):
                            rough_scores(c + 1, 1 - par, u)
                        if m == NT - 2:
                            turn_maxima(c + 1)
                    if m > 0:
                        if m == 1 and not first:
                            pe.wait_ge(epilogue, c * NEPI + 2)
                        weigh(c, m - 1)
                    elif not first:
                        weigh(c - 1, NT - 1)
                        denominators(c - 1)
                    if m == 2 and not first:
                        project(c - 1)
            over_chunks(chunk)(pe)
            weigh(NCH - 1, NT - 1)
            denominators(NCH - 1)
            project(NCH - 1)


def layer1(nc, ctx, T, w1, a12, mask_dram, x1_dram, out):
    def sb(name, shape, dt):
        return ctx.enter_context(nc.sbuf_tensor(name, shape, dt))

    def sem(name):
        return ctx.enter_context(nc.semaphore("l1_" + name))

    values, mask = T["values"], T["mask"]
    ident, ident16, ones = T["ident"], T["ident16"], T["ones"]
    nodes = sb("nodes", [P, NT, D], F32)
    centred = sb("centred", [P, 2, CH], F32)
    ht = sb("ht", [P, 2, CH], F32)
    probs = T["probs"][:, :, 0, :]
    relu = T["probs"][:, :, 1, :]
    w_h = sb("w_h", [P, D], F32)
    w_ht = sb("w_ht", [P, D], F32)
    a_col = sb("a_col", [P, 2], F32)
    w_f = sb("w_f", [P, 2], F32)
    w_fall = sb("w_fall", [P, 2, P], F32)
    f1_all = sb("f1_all", [P, N], F32)
    f2_all = sb("f2_all", [P, N], F32)
    f1_now = sb("f1_now", [P, 2, CH], F32)
    f_col = sb("f_col", [P, NT, 2], F32)
    f2_relu = sb("f2_relu", [P, NT], F32)
    f2_exp = sb("f2_exp", [P, NT], F32)
    arg = sb("arg", [P, 2, CH], F32)
    junk = sb("junk", [P, 4, CH], BF16)
    row_max = sb("row_max1", [P, TPC, GROUPS], F32)
    tops = sb("tops", [P, 4, TPC], F32)
    shift = sb("shift", [P, TPC, 2], F32)
    shift_row = sb("shift_row", [P, 2, CH], F32R)
    shift_high = sb("shift_high", [P, TPC], F32R)
    ones_r = sb("ones_r", [P, P], F32R)
    sums = sb("sums1", [P, CH], F32)
    rden = sb("rden1", [P, CH], F32)
    attended = sb("attended1", [P, CH], F32)
    result = sb("result", [P, CH], F32)

    NS = 2
    scores = [ctx.enter_context(nc.psum_tensor(f"e{b}", [P, CH], F32)) for b in range(NS)]
    weighted = ctx.enter_context(nc.psum_tensor("weighted1", [P, CH], F32))
    misc = ctx.enter_context(nc.psum_tensor("misc1", [P, CH], F32))
    rows = ctx.enter_context(nc.psum_tensor("rows", [P, CH], F32))
    ps_f = ctx.enter_context(nc.psum_tensor("ps_f", [P, CH], F32))
    ps_t = [weighted, misc]
    ps_h, ps_all = rows, scores

    io_done = sem("io")
    w_loaded, consts, w_turned, w_copied, w_folded = (
        sem("w_loaded"), sem("consts"), sem("w_turned"), sem("w_copied"), sem("w_folded"))
    stats_done, var_ready, sqrt_done, norm_chain = sem("stats"), sem("var"), sem("sqrt"), sem("chain")
    centred_ready, turned, ht_ready = sem("centred"), sem("turned"), sem("ht")
    projected, h_done, f_done, all_done = sem("projected"), sem("h"), sem("f"), sem("all")
    f_scaled, f1_taken = sem("f_scaled"), sem("f1_taken")
    mask_loaded = [[sem(f"mask{par}{j}") for j in range(TPC)] for par in range(2)]
    top_done, shift_done, shift_turned, shift_copied = (
        sem("top"), sem("shift"), sem("shift_turned"), sem("shift_row"))
    scores_done, relu_done, arg_done, exp_done, pv_done, sum_done = (
        sem("scores"), sem("relu"), sem("arg"), sem("exp"), sem("pv"), sem("sum"))
    den_done, epilogue, out_turned = sem("den"), sem("epilogue"), sem("out_turned")

    def mask_loads(c, par):
        return (c + (2 - par)) // 2 * 16
    NSH = 7
    NEPI = 3
    out_t = out.rearrange("(t p) d -> p t d", p=P)

    with nc.Block() as block:
        @block.sync
        def _(sp):
            sp.dma_start(nodes[:], x1_dram).then_inc(io_done, 16)
            sp.dma_start(w_h[:], w1).then_inc(w_loaded, 16)
            sp.dma_start(a_col[:], a12).then_inc(w_loaded, 16)

            def load_mask(c, par):
                need(sp, scores_done, (c - 1) * NT)
                for j in range(TPC):
                    sp.dma_start(mask[:, par, j, :], mask_dram[bass.ds(c, 1), :, j, :]
                                 .rearrange("o p m -> (o p) m")).then_inc(mask_loaded[par][j], 16)

            def store(e):
                sp.wait_ge(epilogue, (e + 2) * NEPI)
                sp.dma_start(out_t[:, bass.ds(e * TPC, TPC), :],
                             result[:].rearrange("p (t d) -> p t d", t=TPC)).then_inc(io_done, 16)

            load_mask(0, 0)

            def chunk(c, par):
                first = isinstance(c, int) and c == 0
                more = not isinstance(c, int) or c + 1 < NCH
                if more:
                    load_mask(c + 1, 1 - par)
                if not first:
                    store(c - 1)
            over_chunks(chunk)(sp)
            store(NCH - 1)
            sp.wait_ge(io_done, 16 * (NCH + 1))

        @block.gpsimd
        def _(pool):
            def chunk(c, par):
                for m in range(NT):
                    pool.wait_ge(exp_done, c * NT + (m + 1))
                    if m == 0:
                        need(pool, den_done, c)
                        nc.gpsimd.tensor_tensor(sums[:], probs[:, 0, :],
                                                ones[:, 0:1].broadcast_to([P, CH]), ALU.mult).then_inc(sum_done, 1)
                    else:
                        pool.wait_ge(sum_done, c * NT + m)
                        nc.gpsimd.tensor_tensor(sums[:], sums[:], probs[:, m % 2, :],
                                                ALU.add).then_inc(sum_done, 1)
            over_chunks(chunk)(pool)

        @block.scalar
        def _(act):
            act.wait_ge(var_ready, 1)
            nc.scalar.activation(T["std"][:], T["newton"][:], ACT.Sqrt).then_inc(sqrt_done, 1)
            for k in range(NCH):
                cols = slice(k * CH, (k + 1) * CH)
                act.wait_ge(turned, k + 1)
                need(act, projected, 4 * (k - 1))
                nc.scalar.activation(ht[:, k % 2, :], ps_t[k % 2][:], ACT.Relu).then_inc(ht_ready, 1)
                for w, f_all in enumerate((f1_all, f2_all)):
                    act.wait_ge(projected, 4 * k + 3 + w)
                    nc.scalar.activation(f_all[:, cols], ps_all[w][:], ACT.Copy).then_inc(all_done, 1)

            def copy_shift(c, par):
                act.wait_ge(shift_turned, c + 1)
                nc.scalar.activation(shift_row[0:2, par, :], rows[0:2, :], ACT.Copy).then_inc(shift_copied, 1)

            act.wait_ge(consts, 2)
            copy_shift(0, 0)
            act.wait_ge(f_scaled, 2)
            act.wait_ge(all_done, 2 * NCH)

            def relu_of(c, par, m):
                act.wait_ge(f1_taken, c + 1)
                need(act, arg_done, c * NT + (m - 1))
                nc.scalar.activation(relu[:, m % 2, :], f1_now[:, par, :], ACT.Relu,
                                     bias=f2_relu[:, m:m + 1], scale=1.0 - SLOPE1).then_inc(relu_done, 1)

            def exp_of(c, m):
                s = c * NT + m
                act.wait_ge(arg_done, s + 1)
                need(act, pv_done, s - 1)
                need(act, sum_done, s - 1)
                nc.scalar.activation(probs[:, m % 2, :], arg[:, m % 2, :], ACT.Exp,
                                     bias=f2_exp[:, m:m + 1]).then_inc(exp_done, 1)

            def chunk(c, par):
                more = not isinstance(c, int) or c + 1 < NCH
                nc.scalar.activation(f1_now[:, par, :], f1_all[:, bass.ts(c, CH)],
                                     ACT.Copy).then_inc(f1_taken, 1)
                relu_of(c, par, 0)
                for m in range(NT):
                    if m + 1 < NT:
                        relu_of(c, par, m + 1)
                    exp_of(c, m)
                    if more and m == NT - 2:
                        copy_shift(c + 1, 1 - par)
            over_chunks(chunk)(act)

        @block.vector
        def _(dve):
            chain = chained(dve, norm_chain)
            nc.vector.memset(ones_r[:].bitcast(F32), 1.0).then_inc(consts, 1)
            nc.vector.memset(shift_row[:].bitcast(F32), 0.0).then_inc(consts, 1)
            dve.wait_ge(io_done, 16)
            norm_stats(nc, dve, T, nodes, chain, stats_done, sqrt_done, var_ready)
            dve.wait_ge(w_turned, 1)
            nc.vector.tensor_copy(w_ht[:], rows[:, 0:P]).then_inc(w_copied, 1)
            dve.wait_ge(w_turned, 2)
            nc.vector.tensor_copy(w_f[:], ps_f[:, 0:2]).then_inc(w_copied, 1)
            dve.wait_ge(w_copied, 2)
            for w in range(2):
                nc.vector.tensor_scalar(w_fall[:, w, :], ones[:], w_f[:, w:w + 1], None,
                                        ALU.mult).then_inc(w_folded, 1)

            def centre(k):
                need(dve, turned, k - 1)
                for j in range(TPC):
                    t = k * TPC + j
                    last = nc.vector.tensor_scalar(centred[:, k % 2, j * P:(j + 1) * P], nodes[:, t, :],
                                                   T["moments"][:, t, 0:1], T["rstd"][:, t:t + 1],
                                                   ALU.subtract, ALU.mult)
                last.then_inc(centred_ready, 1)

            centre(0)
            for k in range(NCH):
                if k + 1 < NCH:
                    centre(k + 1)
                tiles = slice(k * TPC, (k + 1) * TPC)
                dve.wait_ge(projected, 4 * k + 1)
                nc.vector.tensor_copy(values[:, tiles, :].rearrange("p t d -> p (t d)"),
                                      ps_h[:]).then_inc(h_done, 1)
                dve.wait_ge(projected, 4 * k + 2)
                nc.vector.tensor_copy(f_col[:, tiles, :].rearrange("p t f -> p (t f)"),
                                      ps_f[:, 0:2 * TPC]).then_inc(f_done, 1)
            dve.wait_ge(f_done, NCH)
            nc.vector.tensor_scalar(f2_relu[:], f_col[:, :, 1], 1.0 - SLOPE1, None, ALU.mult).then_inc(f_scaled, 1)
            nc.vector.tensor_scalar(f2_exp[:], f_col[:, :, 1], SLOPE1, None, ALU.mult).then_inc(f_scaled, 1)
            dve.wait_ge(all_done, 2 * NCH)

            def top_waits(c, par, units):
                for u in units:
                    if u % GROUPS == 0:
                        dve.wait_ge(mask_loaded[par][u // GROUPS], mask_loads(c, par))
                if units:
                    need(dve, top_done, c * UNITS + (units[-1] - 3))

            def top_of(c, par, u):
                j, g = u // GROUPS, u % GROUPS
                nc.vector.tensor_tensor_reduce(
                    out=junk[:, u % 4, :], in0=f2_all[:, g * CH:(g + 1) * CH], in1=mask[:, par, j, g * CH:(g + 1) * CH],
                    scale=1.0, scalar=LOWEST, op0=ALU.add, op1=ALU.max,
                    accum_out=row_max[:, j, g:g + 1]).then_inc(top_done, 1)

            def shift_of(c):
                steps = [0]

                def step(instruction):
                    steps[0] += 1
                    instruction.then_inc(shift_done, 1)
                    dve.wait_ge(shift_done, c * NSH + steps[0])
                f1 = f_col[:, bass.ds(c * TPC, TPC), 0]
                dve.wait_ge(top_done, (c + 1) * UNITS)
                step(nc.vector.tensor_reduce(tops[:, 0, :], row_max[:], AX.X, ALU.max))
                step(nc.vector.tensor_tensor(tops[:, 1, :], tops[:, 0, :], f1, ALU.add))
                step(nc.vector.scalar_tensor_tensor(tops[:, 2, :], tops[:, 1, :], SLOPE1, tops[:, 1, :],
                                                    ALU.mult, ALU.max))
                step(nc.vector.tensor_scalar(tops[:, 3, :], f1, SLOPE1, None, ALU.mult))
                step(nc.vector.tensor_tensor(tops[:, 0, :], tops[:, 3, :], tops[:, 2, :], ALU.subtract))
                step(nc.vector.tensor_copy(shift_high[:], tops[:, 0, :]))
                nc.vector.tensor_copy(shift[:, :, 0], shift_high[:].bitcast(F32))
                nc.vector.tensor_tensor(shift[:, :, 1], tops[:, 0, :], shift_high[:].bitcast(F32),
                                        ALU.subtract).then_inc(shift_done, 1)

            for u in range(UNITS):
                top_waits(0, 0, [u])
                top_of(0, 0, u)
            shift_of(0)
            nc.vector.memset(result[:], 0.0).then_inc(epilogue, NEPI)

            def divide(e):
                before = (e + 1) * NEPI
                dve.wait_ge(den_done, e + 1)
                nc.vector.reciprocal(rden[:], misc[:]).then_inc(epilogue, 1)
                dve.wait_ge(epilogue, before + 1)
                nc.vector.tensor_tensor(attended[:], weighted[:], rden[:], ALU.mult).then_inc(epilogue, 1)

            def residual(e):
                dve.wait_ge(out_turned, e + 1)
                dve.wait_ge(io_done, (e + 1) * 16)
                nc.vector.tensor_tensor(result[:].rearrange("p (t d) -> p t d", t=TPC),
                                        misc[:].rearrange("p (t d) -> p t d", t=TPC),
                                        nodes[:, bass.ds(e * TPC, TPC), :], ALU.add).then_inc(epilogue, 1)

            def chunk(c, par):
                first = isinstance(c, int) and c == 0
                more = not isinstance(c, int) or c + 1 < NCH
                for m in range(NT):
                    if m == 1 and not first:
                        divide(c - 1)
                    if m == 4 and not first:
                        residual(c - 1)
                    dve.wait_ge(relu_done, c * NT + (m + 1))
                    dve.wait_ge(scores_done, c * NT + (m + 1))
                    if more:
                        top_waits(c + 1, 1 - par, units_at(m))
                    need(dve, exp_done, c * NT + (m - 1))
                    nc.vector.tensor_tensor(arg[:, m % 2, :], scores[m % 2][:], relu[:, m % 2, :],
                                            ALU.add).then_inc(arg_done, 1)
                    if more:
                        for u in units_at(m):
                            top_of(c + 1, 1 - par, u)
                        if m == LAST_UNIT_STEP + 1:
                            shift_of(c + 1)
            over_chunks(chunk)(dve)
            divide(NCH - 1)
            residual(NCH - 1)

        @block.tensor
        def _(pe):
            pe.wait_ge(w_loaded, 32)
            nc.tensor.transpose(rows[:, 0:P], w_h[:], ident[:]).then_inc(w_turned, 1)
            pe.wait_ge(w_copied, 1)
            nc.tensor.matmul(ps_f[:, 0:2], w_ht[:], a_col[:], start=True, stop=True).then_inc(w_turned, 1)
            pe.wait_ge(w_folded, 2)

            def turn(k):
                pe.wait_ge(centred_ready, k + 1)
                need(pe, ht_ready, k - 1)
                for j in range(TPC):
                    cols = slice(j * P, (j + 1) * P)
                    last = nc.tensor.transpose(ps_t[k % 2][:, cols], centred[:, k % 2, cols], ident[:])
                last.then_inc(turned, 1)

            turn(0)
            for k in range(NCH):
                if k + 1 < NCH:
                    turn(k + 1)
                pe.wait_ge(ht_ready, k + 1)
                need(pe, h_done, k)
                for j in range(TPC):
                    cols = slice(j * P, (j + 1) * P)
                    last = nc.tensor.matmul(ps_h[:, cols], ht[:, k % 2, cols], w_h[:], start=True, stop=True)
                last.then_inc(projected, 1)
                need(pe, f_done, k)
                for j in range(TPC):
                    last = nc.tensor.matmul(ps_f[:, 2 * j:2 * j + 2], ht[:, k % 2, j * P:(j + 1) * P], w_f[:],
                                            start=True, stop=True)
                last.then_inc(projected, 1)
                for w in range(2):
                    need(pe, all_done, 2 * (k - 1) + w + 1)
                    nc.tensor.matmul(ps_all[w][:], w_fall[:, w, :], ht[:, k % 2, :], start=True,
                                     stop=True).then_inc(projected, 1)

            def turn_shift(c):
                pe.wait_ge(shift_done, (c + 1) * NSH)
                need(pe, shift_copied, c)
                for j in range(TPC):
                    last = nc.tensor.matmul(rows[0:2, j * P:(j + 1) * P], shift[:, j, :], ident[:],
                                            start=True, stop=True)
                last.then_inc(shift_turned, 1)

            pe.wait_ge(h_done, NCH)
            turn_shift(0)

            def score(c, par, m):
                bank = scores[m % 2]
                if m == 0:
                    pe.wait_ge(shift_copied, c + 1)
                    for j in range(TPC):
                        pe.wait_ge(mask_loaded[par][j], mask_loads(c, par))
                need(pe, arg_done, c * NT + (m - 1))
                nc.tensor.matmul(bank[:], ones_r[:], shift_row[:, par, :], start=True, stop=False)
                for j in range(TPC):
                    last = nc.tensor.matmul(bank[:, j * P:(j + 1) * P], mask[:, par, j, m * P:(m + 1) * P],
                                            ident16[:], start=False, stop=(j == TPC - 1))
                last.then_inc(scores_done, 1)

            def weigh(c, m):
                pe.wait_ge(exp_done, c * NT + (m + 1))
                nc.tensor.matmul(weighted[:], values[:, m, :], probs[:, m % 2, :], start=(m == 0),
                                 stop=(m == NT - 1)).then_inc(pv_done, 1)

            def denominators(e):
                pe.wait_ge(sum_done, (e + 1) * NT)
                pe.wait_ge(epilogue, (e + 1) * NEPI)
                nc.tensor.matmul(misc[:], ones[:], sums[:], start=True, stop=True).then_inc(den_done, 1)

            def turn_out(e):
                pe.wait_ge(epilogue, (e + 1) * NEPI + 2)
                for j in range(TPC):
                    cols = slice(j * P, (j + 1) * P)
                    last = nc.tensor.transpose(misc[:, cols], attended[:, cols], ident[:])
                last.then_inc(out_turned, 1)

            def chunk(c, par):
                first = isinstance(c, int) and c == 0
                more = not isinstance(c, int) or c + 1 < NCH
                score(c, par, 0)
                for m in range(NT):
                    if m + 1 < NT:
                        score(c, par, m + 1)
                    if more and m == NT - 2:
                        turn_shift(c + 1)
                    if m == 0 and not first:
                        weigh(c - 1, NT - 1)
                        denominators(c - 1)
                    if m > 0:
                        if m == 1 and not first:
                            pe.wait_ge(epilogue, c * NEPI + 2)
                        weigh(c, m - 1)
                    if m == 2 and not first:
                        turn_out(c - 1)
            over_chunks(chunk)(pe)
            weigh(NCH - 1, NT - 1)
            denominators(NCH - 1)
            turn_out(NCH - 1)


def kernel(x, adj, L0_gnn_Wq, L0_gnn_Wk, L0_gnn_Wv, L0_gnn_weightr, L0_gnn_weightd, L0_gnn_bias,
           L1_gnn_weight, L1_gnn_weight_a1, L1_gnn_weight_a2):
    import numpy as np
    import concourse.bacc as bacc
    from concourse.bass_utils import run_bass_kernel_spmd

    arrays = dict(
        x=np.ascontiguousarray(x), adj=np.ascontiguousarray(adj),
        wq=np.ascontiguousarray(L0_gnn_Wq), wk=np.ascontiguousarray(L0_gnn_Wk),
        wv=np.ascontiguousarray(L0_gnn_Wv),
        wo=np.stack([np.asarray(L0_gnn_weightr), np.asarray(L0_gnn_weightd)]),
        bias=np.ascontiguousarray(L0_gnn_bias), w1=np.ascontiguousarray(L1_gnn_weight),
        a12=np.concatenate([np.asarray(L1_gnn_weight_a1), np.asarray(L1_gnn_weight_a2)], axis=1))
    nc = bacc.Bacc("TRN2", target_bir_lowering=False, num_devices=1)
    args = [nc.dram_tensor(n, a.shape, mybir.dt.from_np(a.dtype), kind="ExternalInput").ap()
            for n, a in arrays.items()]
    out = nc.dram_tensor("out", (N, D), F32, kind="ExternalOutput").ap()
    build(nc, *args, out)
    r = run_bass_kernel_spmd(nc, [arrays], core_ids=[0])
    return r.results[0]["out"]
```

```python
from contextlib import ExitStack

import concourse.bass as bass
from concourse import mybir
from concourse.alu_op_type import AluOpType as ALU

F32 = mybir.dt.float32
F32R = mybir.dt.float32r
BF16 = mybir.dt.bfloat16
I32 = mybir.dt.int32
ACT = mybir.ActivationFunctionType
AX = mybir.AxisListType

P = 128
N = 4096
D = 128
HEADS = 2
DH = D // HEADS
CH = 512
NCH = N // CH
NT = N // P
TPC = CH // P
GROUPS = N // CH
UNITS = TPC * GROUPS
STAGES = 4
EPS = 1e-5
MASKED = -float(2 ** 53)
SCALE = float(DH) ** -0.5
SLOPE0 = 0.01
SLOPE1 = 0.2
LOWEST = -3.0e38

FIRST_UNIT, LAST_UNIT = 4, 28
FIRST_TOP, LAST_TOP = 3, 26
AHEAD = 2


def spread(count, first, last, m):
    return [v for v in range(count) if first + v * (last - first + 1) // count == m]


def halves_at(m):
    return spread(HEADS * UNITS, FIRST_UNIT, LAST_UNIT, m)


def tops_at(m):
    return spread(UNITS, FIRST_TOP, LAST_TOP, m)


def need(engine, semaphore, value):
    if not isinstance(value, int) or value > 0:
        engine.wait_ge(semaphore, value)


def over_chunks(body):
    def run(engine):
        body(0, 0)
        with engine.Fori(0, (NCH - 2) // 2) as i:
            body(i * 2 + 1, 1)
            body(i * 2 + 2, 0)
        body(NCH - 1, (NCH - 1) % 2)
    return run


def build(nc, x, adj, wq, wk, wv, wo, bias, w1, a12, out):
    q_dram = nc.dram_tensor("q_scaled", (D, N), F32, kind="Internal").ap()
    x1_dram = nc.dram_tensor("x1", (P, NT, D), F32, kind="Internal").ap()
    mask_dram = nc.dram_tensor("mask", (NCH, P, TPC, N), BF16, kind="Internal").ap()
    with ExitStack() as keep:
        def sb(name, shape, dt, ctx=keep):
            return ctx.enter_context(nc.sbuf_tensor(name, shape, dt))

        shared = dict(
            values=sb("values", [P, NT, D], F32),
            mask=sb("mask_sb", [P, 2, TPC, N], BF16),
            ident=sb("ident", [P, P], F32),
            ident16=sb("ident16", [P, P], BF16),
            ones=sb("ones", [P, P], F32),
            stats=sb("stats", [P, NT, 6], F32),
            moments=sb("moments", [P, NT, 2], F32),
            rstd=sb("rstd", [P, NT], F32),
            std=sb("std", [P, NT], F32),
            newton=sb("newton", [P, NT], F32),
            probs=sb("probs", [P, 2, HEADS, CH], F32),
        )
        with ExitStack() as ctx:
            layer0(nc, ctx, shared, x, adj, wq, wk, wv, wo, bias, q_dram, mask_dram, x1_dram)
        with ExitStack() as ctx:
            layer1(nc, ctx, shared, w1, a12, mask_dram, x1_dram, out)


def norm_stats(nc, dve, T, nodes, chain, stats_done, sqrt_done, var_ready):
    for t in range(NT):
        last = nc.vector.bn_stats(T["stats"][:, t, :], nodes[:, t, :])
    last.then_inc(stats_done, 1)
    dve.wait_ge(stats_done, 1)
    for t in range(NT):
        last = nc.vector.bn_aggr(T["moments"][:, t, :], T["stats"][:, t, :])
    last.then_inc(stats_done, 1)
    dve.wait_ge(stats_done, 2)
    var = T["moments"][:, :, 1]
    nc.vector.tensor_scalar(T["newton"][:], var, EPS, None, ALU.add).then_inc(var_ready, 1)
    dve.wait_ge(sqrt_done, 1)
    rstd, std, newton = T["rstd"][:], T["std"][:], T["newton"][:]
    chain(nc.vector.reciprocal(rstd, std))
    chain(nc.vector.tensor_tensor(std, rstd, rstd, ALU.mult))
    chain(nc.vector.tensor_tensor(std, std, newton, ALU.mult))
    chain(nc.vector.tensor_scalar(std, std, -0.5, 1.5, ALU.mult, ALU.add))
    chain(nc.vector.tensor_tensor(rstd, rstd, std, ALU.mult))


def chained(dve, semaphore):
    count = [0]

    def chain(instruction):
        count[0] += 1
        instruction.then_inc(semaphore, 1)
        dve.wait_ge(semaphore, count[0])
    return chain


def layer0(nc, ctx, T, x, adj, wq, wk, wv, wo, bias, q_dram, mask_dram, x1_dram):
    def sb(name, shape, dt):
        return ctx.enter_context(nc.sbuf_tensor(name, shape, dt))

    def sem(name):
        return ctx.enter_context(nc.semaphore("l0_" + name))

    values, mask, probs = T["values"], T["mask"], T["probs"]
    ident, ident16, ones = T["ident"], T["ident16"], T["ones"]
    spare = mask[:, 1].rearrange("p t m -> p (t m)").bitcast(F32)
    nodes = spare[:, 0:NT * D].rearrange("p (t d) -> p t d", d=D)
    centred = spare[:, NT * D:NT * D + 2 * CH].rearrange("p (b n) -> p b n", b=2)
    ht = spare[:, NT * D + 2 * CH:NT * D + 4 * CH].rearrange("p (b n) -> p b n", b=2)
    k_split = [sb(f"k_split{h}", [P, N], F32R) for h in range(HEADS)]
    k_one = [sb(f"k_one{h}", [DH + 1, N], F32R) for h in range(HEADS)]
    q_high = [sb(f"q_high{h}", [P, 2, CH], F32R) for h in range(HEADS)]
    q_low = [sb(f"q_low{h}", [DH + 1, 2, CH], F32R) for h in range(HEADS)]
    q_raw = sb("q_raw", [P, HEADS, CH], F32)
    sums = sb("sums", [P, HEADS, CH], F32)
    staged = sb("staged", [P, STAGES, CH], I32)
    row_max = sb("row_max", [P, HEADS, TPC, GROUPS], F32)
    pause = sb("pause", [P, 1], F32)
    top = sb("top", [P, HEADS * TPC], F32)
    neg_max = sb("neg_max", [P, HEADS * TPC, DH + 1], F32)
    w_k = sb("w_k", [P, HEADS, 2 * DH], F32)
    w_q = sb("w_q", [P, D], F32)
    w_v = sb("w_v", [P, D], F32)
    w_now = sb("w_now", [P, D], F32)
    bias_all = sb("bias_all", [P, D], F32)
    y = sb("y", [P, CH], F32)
    y_act = sb("y_act", [P, CH], F32)
    attended = sb("attended", [P, CH], F32)
    rden = sb("rden", [P, HEADS * TPC], F32)
    x_rows = sb("x_rows", [P, CH], F32)

    scores = [ctx.enter_context(nc.psum_tensor(f"scores{b}", [P, HEADS, CH], F32)) for b in range(2)]
    rough = ctx.enter_context(nc.psum_tensor("rough", [P, HEADS, CH], F32))
    weighted = ctx.enter_context(nc.psum_tensor("weighted", [P, CH], F32))
    misc = ctx.enter_context(nc.psum_tensor("misc", [P, CH], F32))

    rough_banks = [rough[:, 0, :], rough[:, 1, :], misc[:]]
    ps_t = [weighted, misc]
    ps_k = [scores[0][:, 0, :], scores[0][:, 1, :]]
    ps_q, ps_v = scores[1][:, 0, :], scores[1][:, 1, :]

    x_loaded, w_loaded, b_loaded = sem("x_loaded"), sem("w_loaded"), sem("b_loaded")
    ident_made, consts = sem("ident"), sem("consts")
    stats_done, var_ready, sqrt_done, norm_chain = sem("stats"), sem("var"), sem("sqrt"), sem("chain")
    centred_ready, turned, ht_ready = sem("centred"), sem("turned"), sem("ht")
    projected, k_high_done, k_done, q_done, v_done = (
        sem("projected"), sem("k_high"), sem("k"), sem("q"), sem("v"))
    q_stored, q_raw_loaded = sem("q_stored"), sem("q_raw")
    q_high_done, q_low_done = sem("q_high"), sem("q_low")
    adj_loaded = [sem(f"adj{s}") for s in range(STAGES)]
    mask_done, mask_stored = sem("mask"), sem("mask_stored")
    rough_done, rough_read = sem("rough"), sem("rough_read")
    max_done, max_turned, max_row = sem("max"), sem("max_turned"), sem("max_row")
    scores_done, exp_done, pv_done = sem("scores"), sem("exp"), sem("pv")
    sum_done = [sem("sum0"), sem("sum1")]
    den_done, epilogue, out_done = sem("den"), sem("epilogue"), sem("out")
    attended_done, k_one_done = sem("attended"), sem("k_one")
    x_rows_loaded, x1_stored = sem("x_rows"), sem("x1_stored")

    x_t = x.rearrange("(c p) d -> p c d", p=P)
    adj_t = adj.rearrange("(c p) m -> c p m", p=P)
    NEPI = 5

    with nc.Block() as block:
        @block.sync
        def _(sp):
            for k in range(NCH):
                sp.dma_start(nodes[:, k * TPC:(k + 1) * TPC, :],
                             x_t[:, k * TPC:(k + 1) * TPC, :]).then_inc(x_loaded, 16)
            for h in range(HEADS):
                for twice in range(2):
                    sp.dma_start(w_k[:, h, twice * DH:(twice + 1) * DH],
                                 wk[:, h * DH:(h + 1) * DH]).then_inc(w_loaded, 16)
            sp.dma_start(w_q[:], wq).then_inc(w_loaded, 16)
            sp.dma_start(w_v[:], wv).then_inc(w_loaded, 16)
            sp.dma_start(bias_all[:], bias.partition_broadcast(P)).then_inc(b_loaded, 16)

            def load_adjacency(c, units=range(UNITS)):
                for u in units:
                    g, j = u // TPC, u % TPC
                    need(sp, mask_done, c * UNITS + (u - STAGES + 1))
                    rows = adj_t[bass.ds(c * TPC + j, 1), :, g * CH:(g + 1) * CH]
                    sp.dma_start(staged[:, u % STAGES, :],
                                 rows.rearrange("o p m -> (o p) m")).then_inc(adj_loaded[u % STAGES], 16)

            def load_q(c):
                need(sp, q_low_done, c * HEADS)
                for h in range(HEADS):
                    for twice in range(2):
                        sp.dma_start(q_raw[twice * DH:(twice + 1) * DH, h, :],
                                     q_dram[h * DH:(h + 1) * DH, bass.ts(c, CH)]).then_inc(q_raw_loaded, 16)

            load_adjacency(0, range(STAGES))
            sp.wait_ge(q_stored, 16)
            load_q(0)
            load_adjacency(0, range(STAGES, UNITS))
            sp.wait_ge(q_stored, 16 * NCH)

            def chunk(c, par):
                sp.wait_ge(mask_done, (c + 1) * UNITS)
                sp.dma_start(mask_dram[bass.ds(c, 1)].rearrange("o p t m -> (o p) t m"),
                             mask[:, par]).then_inc(mask_stored, 16)
                if not isinstance(c, int) or c + 1 < NCH:
                    load_q(c + 1)
                    load_adjacency(c + 1)
                if not isinstance(c, int) or c > 0:
                    store_x1(c - 1)
                load_x(c)

            def store_x1(e):
                sp.wait_ge(epilogue, (e + 2) * NEPI)
                sp.dma_start(x1_dram[:, bass.ds(e * TPC, TPC), :],
                             y[:].rearrange("p (t d) -> p t d", t=TPC)).then_inc(x1_stored, 16)

            def load_x(e):
                need(sp, x1_stored, e * 16)
                sp.dma_start(x_rows[:].rearrange("p (t d) -> p t d", t=TPC),
                             x_t[:, bass.ds(e * TPC, TPC), :]).then_inc(x_rows_loaded, 16)
                sp.dma_start(w_now[:], wo[bass.ds(e // (NCH // 2), 1)]
                             .rearrange("o d e -> (o d) e")).then_inc(x_rows_loaded, 16)
            over_chunks(chunk)(sp)
            store_x1(NCH - 1)
            sp.wait_ge(x1_stored, 16 * NCH)
            sp.wait_ge(mask_stored, 16 * NCH)

        @block.gpsimd
        def _(pool):
            nc.gpsimd.memset(ident[:], 0.0).then_inc(ident_made, 1)
            pool.wait_ge(ident_made, 1)
            nc.gpsimd.affine_select(out=ident[:], in_=ident[:], compare_op=ALU.not_equal, fill=1.0,
                                    base=0, pattern=[[-1, P]], channel_multiplier=1).then_inc(ident_made, 1)
            pool.wait_ge(ident_made, 2)
            nc.gpsimd.tensor_copy(ident16[:], ident[:]).then_inc(consts, 1)
            pool.wait_ge(consts, 5)

            def chunk(c, par):
                for m in range(NT):
                    pool.wait_ge(exp_done, c * NT + (m + 1))
                    if m == 0:
                        need(pool, den_done, c)
                        nc.gpsimd.tensor_tensor(sums[:, 0, :], probs[:, 0, 0, :],
                                                ones[:, 0:1].broadcast_to([P, CH]), ALU.mult).then_inc(sum_done[0], 1)
                    else:
                        pool.wait_ge(sum_done[0], c * NT + m)
                        nc.gpsimd.tensor_tensor(sums[:, 0, :], sums[:, 0, :], probs[:, m % 2, 0, :],
                                                ALU.add).then_inc(sum_done[0], 1)
            over_chunks(chunk)(pool)

        @block.scalar
        def _(act):
            def round_q(c, par):
                act.wait_ge(q_raw_loaded, (c + 1) * 64)
                for h in range(HEADS):
                    nc.scalar.activation(q_high[h][:, par, :], q_raw[:, h, :],
                                         ACT.Copy).then_inc(q_high_done, 1)

            act.wait_ge(var_ready, 1)
            nc.scalar.activation(T["std"][:], T["newton"][:], ACT.Sqrt).then_inc(sqrt_done, 1)
            for k in range(NCH):
                cols = slice(k * CH, (k + 1) * CH)
                act.wait_ge(turned, k + 1)
                need(act, projected, 4 * (k - 1))
                nc.scalar.activation(ht[:, k % 2, :], ps_t[k % 2][:], ACT.Relu).then_inc(ht_ready, 1)
                for h in range(HEADS):
                    act.wait_ge(projected, 4 * k + h + 1)
                    nc.scalar.activation(k_split[h][:, cols], ps_k[h], ACT.Copy).then_inc(k_high_done, 1)
                    nc.scalar.activation(k_one[h][0:DH, cols], ps_k[h][0:DH, :],
                                         ACT.Copy).then_inc(k_one_done, 1)
                act.wait_ge(projected, 4 * k + 3)
                need(act, q_stored, 16 * k)
                nc.scalar.activation(y[:], ps_q, ACT.Copy, scale=SCALE).then_inc(q_done, 1)
                act.wait_ge(q_done, k + 1)
                act.dma_start(q_dram[:, cols], y[:]).then_inc(q_stored, 16)
                act.wait_ge(projected, 4 * k + 4)
                nc.scalar.activation(values[:, k * TPC:(k + 1) * TPC, :].rearrange("p t d -> p (t d)"),
                                     ps_v, ACT.Copy).then_inc(v_done, 1)
                if k == 1:
                    round_q(0, 0)

            def max_rows(c, par):
                act.wait_ge(max_turned, c + 1)
                for h in range(HEADS):
                    nc.scalar.activation(q_low[h][DH:DH + 1, par, :], rough[DH:DH + 1, h, :],
                                         ACT.Copy).then_inc(max_row, 1)

            max_rows(0, 0)

            def chunk(c, par):
                first = isinstance(c, int) and c == 0
                more = not isinstance(c, int) or c + 1 < NCH
                for m in range(NT):
                    s = c * NT + m
                    act.wait_ge(scores_done, s + 1)
                    need(act, pv_done, s - 1)
                    need(act, sum_done[0], s - 1)
                    need(act, sum_done[1], s - 1)
                    nc.scalar.activation(probs[:, m % 2], scores[m % 2][:], ACT.Exp).then_inc(exp_done, 1)
                    if m == 0 and not first:
                        act.wait_ge(pv_done, c * NT)
                        nc.scalar.activation(attended[:], weighted[:], ACT.Copy).then_inc(attended_done, 1)
                    if more and m == 0:
                        round_q(c + 1, 1 - par)
                    if more and m == NT - 2:
                        max_rows(c + 1, 1 - par)
            over_chunks(chunk)(act)
            act.wait_ge(pv_done, NCH * NT)
            nc.scalar.activation(attended[:], weighted[:], ACT.Copy).then_inc(attended_done, 1)

        @block.vector
        def _(dve):
            chain = chained(dve, norm_chain)
            nc.vector.memset(ones[:], 1.0).then_inc(consts, 1)
            for h in range(HEADS):
                nc.vector.memset(k_one[h][DH:DH + 1, :].bitcast(F32), 1.0).then_inc(consts, 1)
            nc.vector.memset(neg_max[:], 0.0).then_inc(consts, 1)
            dve.wait_ge(x_loaded, 16 * NCH)
            norm_stats(nc, dve, T, nodes, chain, stats_done, sqrt_done, var_ready)

            def centre(k):
                need(dve, turned, k - 1)
                for j in range(TPC):
                    t = k * TPC + j
                    last = nc.vector.tensor_scalar(centred[:, k % 2, j * P:(j + 1) * P], nodes[:, t, :],
                                                   T["moments"][:, t, 0:1], T["rstd"][:, t:t + 1],
                                                   ALU.subtract, ALU.mult)
                last.then_inc(centred_ready, 1)

            def convert(c, par, u):
                if u == UNITS:
                    nc.vector.memset(pause[:], 0.0)
                    return
                g, j = u // TPC, u % TPC
                dve.wait_ge(adj_loaded[u % STAGES], (c * GROUPS + (g + 1)) * 16)
                nc.vector.tensor_scalar(mask[:, par, j, g * CH:(g + 1) * CH], staged[:, u % STAGES, :],
                                        0.0, MASKED, ALU.is_le, ALU.mult).then_inc(mask_done, 1)

            def top_of(c, par, u, banks=3):
                g, j = u // TPC, u % TPC
                dve.wait_ge(mask_done, c * UNITS + (u + 1))
                dve.wait_ge(rough_done, (c * UNITS + (u + 1)) * HEADS)
                convert(c, par, u + 1)
                for h in range(HEADS):
                    bank = rough_banks[(HEADS * u + h) % banks]
                    nc.vector.tensor_tensor_reduce(
                        out=bank, in0=bank, in1=mask[:, par, j, g * CH:(g + 1) * CH],
                        scale=1.0, scalar=LOWEST, op0=ALU.add, op1=ALU.max,
                        accum_out=row_max[:, h, j, g:g + 1]).then_inc(rough_read, 1)

            def maxima(c):
                dve.wait_ge(rough_read, (c + 1) * UNITS * HEADS)
                nc.vector.tensor_reduce(top[:], row_max[:].rearrange("p h j g -> p (h j) g"), AX.X,
                                        ALU.max).then_inc(max_done, 1)
                dve.wait_ge(max_done, c * 2 + 1)
                nc.vector.tensor_scalar(neg_max[:, :, DH], top[:], -1.0, None,
                                        ALU.mult).then_inc(max_done, 1)

            def lower_q(c, par):
                for h in range(HEADS):
                    dve.wait_ge(q_high_done, c * HEADS + (h + 1))
                    nc.vector.tensor_tensor(q_low[h][0:DH, par, :], q_raw[0:DH, h, :],
                                            q_high[h][0:DH, par, :].bitcast(F32),
                                            ALU.subtract).then_inc(q_low_done, 1)

            centre(0)
            for k in range(NCH):
                cols = slice(k * CH, (k + 1) * CH)
                if k + 1 < NCH:
                    centre(k + 1)
                for h in range(HEADS):
                    dve.wait_ge(k_high_done, HEADS * k + h + 1)
                    nc.vector.tensor_tensor(k_split[h][DH:P, cols], ps_k[h][DH:P, :],
                                            k_split[h][DH:P, cols].bitcast(F32),
                                            ALU.subtract).then_inc(k_done, 1)
                if k == 0:
                    convert(0, 0, 0)
                if k == 1:
                    lower_q(0, 0)
                for u in range((k - 2) * TPC, (k - 1) * TPC):
                    if u >= 0:
                        top_of(0, 0, u, banks=2)
            for u in range((GROUPS - 2) * TPC, UNITS):
                top_of(0, 0, u, banks=2)
            dve.wait_ge(consts, 5)
            maxima(0)
            nc.vector.memset(y_act[:], 0.0).then_inc(epilogue, NEPI)

            def sum_head1(c, m):
                dve.wait_ge(exp_done, c * NT + (m + 1))
                if m == 0:
                    need(dve, den_done, c)
                    nc.vector.tensor_copy(sums[:, 1, :], probs[:, 0, 1, :]).then_inc(sum_done[1], 1)
                else:
                    dve.wait_ge(sum_done[1], c * NT + m)
                    nc.vector.tensor_tensor(sums[:, 1, :], sums[:, 1, :], probs[:, m % 2, 1, :],
                                            ALU.add).then_inc(sum_done[1], 1)

            def finish(e):
                before = (e + 1) * NEPI
                dve.wait_ge(den_done, e + 1)
                nc.vector.reciprocal(rden[:], misc[:, 0:HEADS * TPC]).then_inc(epilogue, 1)
                dve.wait_ge(x_rows_loaded, (e + 1) * 32)
                dve.wait_ge(out_done, e + 1)
                dve.wait_ge(epilogue, before + 1)
                for h in range(HEADS):
                    for j in range(TPC):
                        cols = slice(j * P, (j + 1) * P)
                        last = nc.vector.scalar_tensor_tensor(
                            y[:, cols], rough[:, h, cols], rden[:, h * TPC + j:h * TPC + j + 1],
                            y[:, cols] if h else bias_all[:], ALU.mult, ALU.add)
                    last.then_inc(epilogue, 1)
                    dve.wait_ge(epilogue, before + (2 + h))
                nc.vector.scalar_tensor_tensor(y_act[:], y[:], SLOPE0, y[:], ALU.mult,
                                               ALU.max).then_inc(epilogue, 1)
                dve.wait_ge(epilogue, before + 4)
                nc.vector.tensor_tensor(y[:], x_rows[:], y_act[:], ALU.add).then_inc(epilogue, 1)

            def chunk(c, par):
                first = isinstance(c, int) and c == 0
                more = not isinstance(c, int) or c + 1 < NCH
                for m in range(NT):
                    if m > 0:
                        sum_head1(c, m - 1)
                    if m == 1 and more:
                        need(dve, scores_done, c * NT)
                        lower_q(c + 1, 1 - par)
                    if m == 3 and not first:
                        finish(c - 1)
                    if more:
                        if m == FIRST_UNIT:
                            need(dve, mask_stored, c * 16)
                            convert(c + 1, 1 - par, 0)
                        for v in halves_at(m):
                            if v % HEADS == HEADS - 1:
                                top_of(c + 1, 1 - par, v // HEADS)
                        if m == LAST_UNIT + 1:
                            maxima(c + 1)
                sum_head1(c, NT - 1)
            over_chunks(chunk)(dve)
            finish(NCH - 1)

        @block.tensor
        def _(pe):
            pe.wait_ge(consts, 5)
            pe.wait_ge(w_loaded, 16 * 6)
            pe.wait_ge(b_loaded, 16)

            def turn(k):
                pe.wait_ge(centred_ready, k + 1)
                need(pe, ht_ready, k - 1)
                for j in range(TPC):
                    cols = slice(j * P, (j + 1) * P)
                    last = nc.tensor.transpose(ps_t[k % 2][:, cols], centred[:, k % 2, cols], ident[:])
                last.then_inc(turned, 1)

            def rough_scores(c, par, v, banks=3):
                u, h = v // HEADS, v % HEADS
                g, j = u // TPC, u % TPC
                if v >= banks:
                    pe.wait_ge(rough_read, c * UNITS * HEADS + (v - banks + 1))
                nc.tensor.matmul(rough_banks[v % banks], q_high[h][:, par, j * P:(j + 1) * P],
                                 k_split[h][:, g * CH:(g + 1) * CH], start=True,
                                 stop=True).then_inc(rough_done, 1)

            def turn_maxima(c):
                pe.wait_ge(max_done, (c + 1) * 2)
                for h in range(HEADS):
                    for j in range(TPC):
                        last = nc.tensor.matmul(rough[0:DH + 1, h, j * P:(j + 1) * P],
                                                neg_max[:, h * TPC + j, :], ident[:], start=True, stop=True)
                last.then_inc(max_turned, 1)

            turn(0)
            for k in range(NCH):
                if k == 2:
                    pe.wait_ge(q_high_done, HEADS)
                if k + 1 < NCH:
                    turn(k + 1)
                pe.wait_ge(ht_ready, k + 1)
                for h in range(HEADS):
                    need(pe, k_done, HEADS * (k - 1) + h + 1)
                    need(pe, k_one_done, HEADS * (k - 1) + h + 1)
                    nc.tensor.matmul(ps_k[h], w_k[:, h, :], ht[:, k % 2, :], start=True,
                                     stop=True).then_inc(projected, 1)
                need(pe, q_done, k)
                nc.tensor.matmul(ps_q, w_q[:], ht[:, k % 2, :], start=True, stop=True).then_inc(projected, 1)
                need(pe, v_done, k)
                for j in range(TPC):
                    cols = slice(j * P, (j + 1) * P)
                    last = nc.tensor.matmul(ps_v[:, cols], ht[:, k % 2, cols], w_v[:], start=True, stop=True)
                last.then_inc(projected, 1)
                for v in range((k - 2) * TPC * HEADS, (k - 1) * TPC * HEADS):
                    if v >= 0:
                        rough_scores(0, 0, v, banks=2)
            pe.wait_ge(k_done, HEADS * NCH)
            for v in range((GROUPS - 2) * TPC * HEADS, UNITS * HEADS):
                rough_scores(0, 0, v, banks=2)
            pe.wait_ge(k_one_done, HEADS * NCH)
            pe.wait_ge(v_done, NCH)
            turn_maxima(0)

            def score(c, par, m):
                s = c * NT + m
                keys = slice(m * P, (m + 1) * P)
                bank = scores[m % 2]
                if m == 0:
                    pe.wait_ge(q_high_done, (c + 1) * HEADS)
                need(pe, exp_done, s - 1)
                for h in range(HEADS):
                    nc.tensor.matmul(bank[:, h, :], k_split[h][:, keys], q_high[h][:, par, :],
                                     start=True, stop=False)
                if m == 0:
                    pe.wait_ge(mask_done, (c + 1) * UNITS)
                for j in range(TPC):
                    for h in range(HEADS):
                        nc.tensor.matmul(bank[:, h, j * P:(j + 1) * P], mask[:, par, j, keys], ident16[:],
                                         start=False, stop=False)
                if m == 0:
                    pe.wait_ge(q_low_done, (c + 1) * HEADS)
                    pe.wait_ge(max_row, (c + 1) * HEADS)
                for h in range(HEADS):
                    last = nc.tensor.matmul(bank[:, h, :], k_one[h][:, keys], q_low[h][:, par, :],
                                            start=False, stop=True)
                last.then_inc(scores_done, 1)

            def weigh(c, m):
                pe.wait_ge(exp_done, c * NT + (m + 1))
                for h in range(HEADS):
                    last = nc.tensor.matmul(weighted[h * DH:(h + 1) * DH, :],
                                            values[:, m, h * DH:(h + 1) * DH], probs[:, m % 2, h, :],
                                            start=(m == 0), stop=(m == NT - 1))
                last.then_inc(pv_done, 1)

            def denominators(e):
                pe.wait_ge(sum_done[0], (e + 1) * NT)
                pe.wait_ge(sum_done[1], (e + 1) * NT)
                pe.wait_ge(epilogue, (e + 1) * NEPI)
                for h in range(HEADS):
                    for j in range(TPC):
                        o = h * TPC + j
                        last = nc.tensor.matmul(misc[:, o:o + 1], sums[:, h, j * P:(j + 1) * P],
                                                ones[:, 0:1], start=True, stop=True)
                last.then_inc(den_done, 1)

            def project(e):
                pe.wait_ge(x_rows_loaded, (e + 1) * 32)
                for h in range(HEADS):
                    dims = slice(h * DH, (h + 1) * DH)
                    for j in range(TPC):
                        cols = slice(j * P, (j + 1) * P)
                        last = nc.tensor.matmul(rough[:, h, cols], attended[dims, cols],
                                                w_now[dims, :], start=True, stop=True)
                last.then_inc(out_done, 1)

            def chunk(c, par):
                first = isinstance(c, int) and c == 0
                more = not isinstance(c, int) or c + 1 < NCH
                for m in range(NT):
                    score(c, par, m)
                    if more:
                        if m == FIRST_UNIT:
                            pe.wait_ge(q_high_done, (c + 2) * HEADS)
                            if not first:
                                pe.wait_ge(epilogue, (c + 1) * NEPI)
                        if m == NT - 2:
                            turn_maxima(c + 1)
                        for v in halves_at(m)[:1]:
                            rough_scores(c + 1, 1 - par, v)
                    if m == 0 and not first:
                        weigh(c - 1, NT - 1)
                    if m == 1 and not first:
                        denominators(c - 1)
                        pe.wait_ge(attended_done, c)
                    if m > 0:
                        weigh(c, m - 1)
                    if m == 2 and not first:
                        project(c - 1)
                    if more:
                        for v in halves_at(m)[1:]:
                            rough_scores(c + 1, 1 - par, v)
            over_chunks(chunk)(pe)
            weigh(NCH - 1, NT - 1)
            denominators(NCH - 1)
            pe.wait_ge(attended_done, NCH)
            project(NCH - 1)


def layer1(nc, ctx, T, w1, a12, mask_dram, x1_dram, out):
    def sb(name, shape, dt):
        return ctx.enter_context(nc.sbuf_tensor(name, shape, dt))

    def sem(name):
        return ctx.enter_context(nc.semaphore("l1_" + name))

    values, mask = T["values"], T["mask"]
    ident, ident16, ones = T["ident"], T["ident16"], T["ones"]
    nodes = sb("nodes", [P, NT, D], F32)
    centred = sb("centred", [P, 2, CH], F32)
    ht = sb("ht", [P, 2, CH], F32)
    RING = 4
    probs = T["probs"][:].rearrange("p a b n -> p (a b) n")
    relu = sb("relu", [P, RING, CH], F32)
    w_h = sb("w_h", [P, D], F32)
    w_ht = sb("w_ht", [P, D], F32)
    a_col = sb("a_col", [P, 2], F32)
    w_f = sb("w_f", [P, 2], F32)
    w_fall = sb("w_fall", [P, 2, P], F32)
    f1_all = sb("f1_all", [P, N], F32)
    f2_all = sb("f2_all", [P, N], F32)
    f1_now = sb("f1_now", [P, 2, CH], F32)
    f_col = sb("f_col", [P, NT, 2], F32)
    f2_relu = sb("f2_relu", [P, NT], F32)
    f2_exp = sb("f2_exp", [P, NT], F32)
    arg = sb("arg", [P, RING, CH], F32)
    junk = sb("junk", [P, 4, CH], BF16)
    row_max = sb("row_max1", [P, TPC, GROUPS], F32)
    tops = sb("tops", [P, 4, TPC], F32)
    shift = sb("shift", [P, TPC, 2], F32)
    shift_row = sb("shift_row", [P, 2, CH], F32R)
    shift_high = sb("shift_high", [P, TPC], F32R)
    ones_r = sb("ones_r", [P, P], F32R)
    sums = sb("sums1", [P, CH], F32)
    rden = sb("rden1", [P, TPC], F32)
    attended = sb("attended1", [P, CH], F32)
    result = sb("result", [P, CH], F32)

    scores = [ctx.enter_context(nc.psum_tensor(f"e{b}", [P, CH], F32)) for b in range(RING)]
    weighted = ctx.enter_context(nc.psum_tensor("weighted1", [P, CH], F32))
    misc = ctx.enter_context(nc.psum_tensor("misc1", [P, CH], F32))
    rows = ctx.enter_context(nc.psum_tensor("rows", [P, CH], F32))
    ps_f = ctx.enter_context(nc.psum_tensor("ps_f", [P, CH], F32))
    ps_t = [weighted, misc]
    ps_h, ps_all = rows, scores

    io_done = sem("io")
    w_loaded, consts, w_turned, w_copied, w_folded = (
        sem("w_loaded"), sem("consts"), sem("w_turned"), sem("w_copied"), sem("w_folded"))
    stats_done, var_ready, sqrt_done, norm_chain = sem("stats"), sem("var"), sem("sqrt"), sem("chain")
    centred_ready, turned, ht_ready = sem("centred"), sem("turned"), sem("ht")
    projected, h_done, f_done, all_done = sem("projected"), sem("h"), sem("f"), sem("all")
    f_scaled, f1_taken = sem("f_scaled"), sem("f1_taken")
    mask_loaded = [[sem(f"mask{par}{j}") for j in range(TPC)] for par in range(2)]
    top_done, shift_done, shift_turned, shift_copied = (
        sem("top"), sem("shift"), sem("shift_turned"), sem("shift_row"))
    scores_done, relu_done, arg_done, exp_done, pv_done, sum_done = (
        sem("scores"), sem("relu"), sem("arg"), sem("exp"), sem("pv"), sem("sum"))
    attended_done = sem("attended")
    den_done, epilogue, out_turned = sem("den"), sem("epilogue"), sem("out_turned")

    def mask_loads(c, par):
        return (c + (2 - par)) // 2 * 16
    NSH = 7
    NEPI = 2
    out_t = out.rearrange("(t p) d -> p t d", p=P)

    with nc.Block() as block:
        @block.sync
        def _(sp):
            sp.dma_start(nodes[:], x1_dram).then_inc(io_done, 16)
            sp.dma_start(w_h[:], w1).then_inc(w_loaded, 16)
            sp.dma_start(a_col[:], a12).then_inc(w_loaded, 16)

            def load_mask(c, par):
                need(sp, scores_done, (c - 1) * NT)
                for j in range(TPC):
                    sp.dma_start(mask[:, par, j, :], mask_dram[bass.ds(c, 1), :, j, :]
                                 .rearrange("o p m -> (o p) m")).then_inc(mask_loaded[par][j], 16)

            def store(e):
                sp.wait_ge(epilogue, (e + 2) * NEPI)
                sp.dma_start(out_t[:, bass.ds(e * TPC, TPC), :],
                             result[:].rearrange("p (t d) -> p t d", t=TPC)).then_inc(io_done, 16)

            load_mask(0, 0)

            def chunk(c, par):
                first = isinstance(c, int) and c == 0
                more = not isinstance(c, int) or c + 1 < NCH
                if more:
                    load_mask(c + 1, 1 - par)
                if not first:
                    store(c - 1)
            over_chunks(chunk)(sp)
            store(NCH - 1)
            sp.wait_ge(io_done, 16 * (NCH + 1))

        @block.gpsimd
        def _(pool):
            def chunk(c, par):
                for m in range(NT):
                    pool.wait_ge(exp_done, c * NT + (m + 1))
                    if m == 0:
                        need(pool, den_done, c)
                        nc.gpsimd.tensor_tensor(sums[:], probs[:, 0, :],
                                                ones[:, 0:1].broadcast_to([P, CH]), ALU.mult).then_inc(sum_done, 1)
                    else:
                        pool.wait_ge(sum_done, c * NT + m)
                        nc.gpsimd.tensor_tensor(sums[:], sums[:], probs[:, m % RING, :],
                                                ALU.add).then_inc(sum_done, 1)
            over_chunks(chunk)(pool)

        @block.scalar
        def _(act):
            act.wait_ge(var_ready, 1)
            nc.scalar.activation(T["std"][:], T["newton"][:], ACT.Sqrt).then_inc(sqrt_done, 1)
            for k in range(NCH):
                cols = slice(k * CH, (k + 1) * CH)
                act.wait_ge(turned, k + 1)
                need(act, projected, 4 * (k - 1))
                nc.scalar.activation(ht[:, k % 2, :], ps_t[k % 2][:], ACT.Relu).then_inc(ht_ready, 1)
                for w, f_all in enumerate((f1_all, f2_all)):
                    act.wait_ge(projected, 4 * k + 3 + w)
                    nc.scalar.activation(f_all[:, cols], ps_all[w][:], ACT.Copy).then_inc(all_done, 1)

            def copy_shift(c, par):
                act.wait_ge(shift_turned, c + 1)
                nc.scalar.activation(shift_row[0:2, par, :], rows[0:2, :], ACT.Copy).then_inc(shift_copied, 1)

            act.wait_ge(consts, 2)
            copy_shift(0, 0)
            act.wait_ge(f_scaled, 2)
            act.wait_ge(all_done, 2 * NCH)

            def take_f1(c, par):
                nc.scalar.activation(f1_now[:, par, :], f1_all[:, bass.ts(c, CH)],
                                     ACT.Copy).then_inc(f1_taken, 1)

            def relu_of(c, par, m):
                act.wait_ge(f1_taken, c + 1)
                need(act, arg_done, c * NT + (m - RING + 1))
                nc.scalar.activation(relu[:, m % RING, :], f1_now[:, par, :], ACT.Relu,
                                     bias=f2_relu[:, m:m + 1], scale=1.0 - SLOPE1).then_inc(relu_done, 1)

            def exp_of(c, m):
                s = c * NT + m
                act.wait_ge(arg_done, s + 1)
                need(act, pv_done, s - RING + 1)
                need(act, sum_done, s - RING + 1)
                nc.scalar.activation(probs[:, m % RING, :], arg[:, m % RING, :], ACT.Exp,
                                     bias=f2_exp[:, m:m + 1]).then_inc(exp_done, 1)

            take_f1(0, 0)
            for m in range(AHEAD):
                relu_of(0, 0, m)

            def chunk(c, par):
                first = isinstance(c, int) and c == 0
                more = not isinstance(c, int) or c + 1 < NCH
                for m in range(NT):
                    if m + AHEAD < NT:
                        relu_of(c, par, m + AHEAD)
                    elif more:
                        if m + AHEAD == NT:
                            take_f1(c + 1, 1 - par)
                        relu_of(c + 1, 1 - par, m + AHEAD - NT)
                    exp_of(c, m)
                    if m == 0 and not first:
                        act.wait_ge(pv_done, c * NT)
                        nc.scalar.activation(attended[:], weighted[:], ACT.Copy).then_inc(attended_done, 1)
                    if more and m == LAST_TOP + 2:
                        copy_shift(c + 1, 1 - par)
            over_chunks(chunk)(act)
            act.wait_ge(pv_done, NCH * NT)
            nc.scalar.activation(attended[:], weighted[:], ACT.Copy).then_inc(attended_done, 1)

        @block.vector
        def _(dve):
            chain = chained(dve, norm_chain)
            nc.vector.memset(ones_r[:].bitcast(F32), 1.0).then_inc(consts, 1)
            nc.vector.memset(shift_row[:].bitcast(F32), 0.0).then_inc(consts, 1)
            dve.wait_ge(io_done, 16)
            norm_stats(nc, dve, T, nodes, chain, stats_done, sqrt_done, var_ready)
            dve.wait_ge(w_turned, 1)
            nc.vector.tensor_copy(w_ht[:], rows[:, 0:P]).then_inc(w_copied, 1)
            dve.wait_ge(w_turned, 2)
            nc.vector.tensor_copy(w_f[:], ps_f[:, 0:2]).then_inc(w_copied, 1)
            dve.wait_ge(w_copied, 2)
            for w in range(2):
                nc.vector.tensor_scalar(w_fall[:, w, :], ones[:], w_f[:, w:w + 1], None,
                                        ALU.mult).then_inc(w_folded, 1)

            def centre(k):
                need(dve, turned, k - 1)
                for j in range(TPC):
                    t = k * TPC + j
                    last = nc.vector.tensor_scalar(centred[:, k % 2, j * P:(j + 1) * P], nodes[:, t, :],
                                                   T["moments"][:, t, 0:1], T["rstd"][:, t:t + 1],
                                                   ALU.subtract, ALU.mult)
                last.then_inc(centred_ready, 1)

            def top_waits(c, par, units, first):
                for u in units:
                    if u % GROUPS == 0:
                        dve.wait_ge(mask_loaded[par][u // GROUPS], mask_loads(c, par))
                if units:
                    need(dve, top_done, c * UNITS + (first + len(units) - 4))

            def top_of(c, par, u, slot):
                j, g = u // GROUPS, u % GROUPS
                nc.vector.tensor_tensor_reduce(
                    out=junk[:, slot % 4, :], in0=f2_all[:, g * CH:(g + 1) * CH], in1=mask[:, par, j, g * CH:(g + 1) * CH],
                    scale=1.0, scalar=LOWEST, op0=ALU.add, op1=ALU.max,
                    accum_out=row_max[:, j, g:g + 1]).then_inc(top_done, 1)

            centre(0)
            for k in range(NCH):
                if k + 1 < NCH:
                    centre(k + 1)
                tiles = slice(k * TPC, (k + 1) * TPC)
                dve.wait_ge(projected, 4 * k + 1)
                nc.vector.tensor_copy(values[:, tiles, :].rearrange("p t d -> p (t d)"),
                                      ps_h[:]).then_inc(h_done, 1)
                dve.wait_ge(projected, 4 * k + 2)
                nc.vector.tensor_copy(f_col[:, tiles, :].rearrange("p t f -> p (t f)"),
                                      ps_f[:, 0:2 * TPC]).then_inc(f_done, 1)
                if k > 0:
                    dve.wait_ge(all_done, 2 * k)
                    for j in range(TPC):
                        u = j * GROUPS + k - 1
                        top_waits(0, 0, [u], (k - 1) * TPC + j)
                        top_of(0, 0, u, (k - 1) * TPC + j)
            dve.wait_ge(all_done, 2 * NCH)
            for j in range(TPC):
                u = j * GROUPS + GROUPS - 1
                top_waits(0, 0, [u], (GROUPS - 1) * TPC + j)
                top_of(0, 0, u, (GROUPS - 1) * TPC + j)
            dve.wait_ge(f_done, NCH)
            nc.vector.tensor_scalar(f2_relu[:], f_col[:, :, 1], 1.0 - SLOPE1, None, ALU.mult).then_inc(f_scaled, 1)
            nc.vector.tensor_scalar(f2_exp[:], f_col[:, :, 1], SLOPE1, None, ALU.mult).then_inc(f_scaled, 1)

            def shift_of(c):
                steps = [0]

                def step(instruction):
                    steps[0] += 1
                    instruction.then_inc(shift_done, 1)
                    dve.wait_ge(shift_done, c * NSH + steps[0])
                f1 = f_col[:, bass.ds(c * TPC, TPC), 0]
                dve.wait_ge(top_done, (c + 1) * UNITS)
                step(nc.vector.tensor_reduce(tops[:, 0, :], row_max[:], AX.X, ALU.max))
                step(nc.vector.tensor_tensor(tops[:, 1, :], tops[:, 0, :], f1, ALU.add))
                step(nc.vector.scalar_tensor_tensor(tops[:, 2, :], tops[:, 1, :], SLOPE1, tops[:, 1, :],
                                                    ALU.mult, ALU.max))
                step(nc.vector.tensor_scalar(tops[:, 3, :], f1, SLOPE1, None, ALU.mult))
                step(nc.vector.tensor_tensor(tops[:, 0, :], tops[:, 3, :], tops[:, 2, :], ALU.subtract))
                step(nc.vector.tensor_copy(shift_high[:], tops[:, 0, :]))
                nc.vector.tensor_copy(shift[:, :, 0], shift_high[:].bitcast(F32))
                nc.vector.tensor_tensor(shift[:, :, 1], tops[:, 0, :], shift_high[:].bitcast(F32),
                                        ALU.subtract).then_inc(shift_done, 1)

            shift_of(0)
            nc.vector.memset(result[:], 0.0).then_inc(epilogue, NEPI)

            def finish(e):
                dve.wait_ge(den_done, e + 1)
                nc.vector.reciprocal(rden[:], misc[:, 0:TPC]).then_inc(epilogue, 1)
                dve.wait_ge(out_turned, e + 1)
                dve.wait_ge(io_done, (e + 1) * 16)
                dve.wait_ge(epilogue, (e + 1) * NEPI + 1)
                for j in range(TPC):
                    cols = slice(j * P, (j + 1) * P)
                    last = nc.vector.scalar_tensor_tensor(result[:, cols], rows[:, cols], rden[:, j:j + 1],
                                                          nodes[:, bass.ds(e * TPC + j, 1), :]
                                                          .rearrange("p o d -> p (o d)"),
                                                          ALU.mult, ALU.add)
                last.then_inc(epilogue, 1)

            def chunk(c, par):
                first = isinstance(c, int) and c == 0
                more = not isinstance(c, int) or c + 1 < NCH
                for m in range(NT):
                    if m == 4 and not first:
                        finish(c - 1)
                    tops = tops_at(m) if more else []
                    dve.wait_ge(relu_done, c * NT + (m + 1))
                    dve.wait_ge(scores_done, c * NT + (m + 1))
                    top_waits(c + 1, 1 - par, tops, tops[0] if tops else 0)
                    need(dve, exp_done, c * NT + (m - RING + 1))
                    nc.vector.tensor_tensor(arg[:, m % RING, :], scores[m % RING][:], relu[:, m % RING, :],
                                            ALU.add).then_inc(arg_done, 1)
                    for u in tops:
                        top_of(c + 1, 1 - par, u, u)
                    if more and m == LAST_TOP + 1:
                        shift_of(c + 1)
            over_chunks(chunk)(dve)
            finish(NCH - 1)

        @block.tensor
        def _(pe):
            pe.wait_ge(w_loaded, 32)
            nc.tensor.transpose(rows[:, 0:P], w_h[:], ident[:]).then_inc(w_turned, 1)
            pe.wait_ge(w_copied, 1)
            nc.tensor.matmul(ps_f[:, 0:2], w_ht[:], a_col[:], start=True, stop=True).then_inc(w_turned, 1)
            pe.wait_ge(w_folded, 2)

            def turn(k):
                pe.wait_ge(centred_ready, k + 1)
                need(pe, ht_ready, k - 1)
                for j in range(TPC):
                    cols = slice(j * P, (j + 1) * P)
                    last = nc.tensor.transpose(ps_t[k % 2][:, cols], centred[:, k % 2, cols], ident[:])
                last.then_inc(turned, 1)

            turn(0)
            for k in range(NCH):
                if k + 1 < NCH:
                    turn(k + 1)
                pe.wait_ge(ht_ready, k + 1)
                need(pe, h_done, k)
                for j in range(TPC):
                    cols = slice(j * P, (j + 1) * P)
                    last = nc.tensor.matmul(ps_h[:, cols], ht[:, k % 2, cols], w_h[:], start=True, stop=True)
                last.then_inc(projected, 1)
                need(pe, f_done, k)
                for j in range(TPC):
                    last = nc.tensor.matmul(ps_f[:, 2 * j:2 * j + 2], ht[:, k % 2, j * P:(j + 1) * P], w_f[:],
                                            start=True, stop=True)
                last.then_inc(projected, 1)
                for w in range(2):
                    need(pe, all_done, 2 * (k - 1) + w + 1)
                    nc.tensor.matmul(ps_all[w][:], w_fall[:, w, :], ht[:, k % 2, :], start=True,
                                     stop=True).then_inc(projected, 1)

            def turn_shift(c):
                pe.wait_ge(shift_done, (c + 1) * NSH)
                need(pe, shift_copied, c)
                for j in range(TPC):
                    last = nc.tensor.matmul(rows[0:2, j * P:(j + 1) * P], shift[:, j, :], ident[:],
                                            start=True, stop=True)
                last.then_inc(shift_turned, 1)

            pe.wait_ge(h_done, NCH)
            turn_shift(0)

            def score(c, par, m):
                bank = scores[m % RING]
                if m == 0:
                    pe.wait_ge(shift_copied, c + 1)
                    for j in range(TPC):
                        pe.wait_ge(mask_loaded[par][j], mask_loads(c, par))
                need(pe, arg_done, c * NT + (m - RING + 1))
                nc.tensor.matmul(bank[:], ones_r[:], shift_row[:, par, :], start=True, stop=False)
                for j in range(TPC):
                    last = nc.tensor.matmul(bank[:, j * P:(j + 1) * P], mask[:, par, j, m * P:(m + 1) * P],
                                            ident16[:], start=False, stop=(j == TPC - 1))
                last.then_inc(scores_done, 1)

            def weigh(c, m):
                pe.wait_ge(exp_done, c * NT + (m + 1))
                nc.tensor.matmul(weighted[:], values[:, m, :], probs[:, m % RING, :], start=(m == 0),
                                 stop=(m == NT - 1)).then_inc(pv_done, 1)

            def denominators(e):
                pe.wait_ge(sum_done, (e + 1) * NT)
                pe.wait_ge(epilogue, (e + 1) * NEPI)
                for j in range(TPC):
                    last = nc.tensor.matmul(misc[:, j:j + 1], sums[:, j * P:(j + 1) * P], ones[:, 0:1],
                                            start=True, stop=True)
                last.then_inc(den_done, 1)

            def turn_out(e):
                for j in range(TPC):
                    cols = slice(j * P, (j + 1) * P)
                    last = nc.tensor.transpose(rows[:, cols], attended[:, cols], ident[:])
                last.then_inc(out_turned, 1)

            for m in range(AHEAD):
                score(0, 0, m)

            def chunk(c, par):
                first = isinstance(c, int) and c == 0
                more = not isinstance(c, int) or c + 1 < NCH
                for m in range(NT):
                    if m + AHEAD < NT:
                        score(c, par, m + AHEAD)
                    elif more:
                        score(c + 1, 1 - par, m + AHEAD - NT)
                    if more and m == LAST_TOP + 2:
                        turn_shift(c + 1)
                    if m == 0 and not first:
                        weigh(c - 1, NT - 1)
                    if m == 1 and not first:
                        denominators(c - 1)
                        pe.wait_ge(attended_done, c)
                    if m > 0:
                        weigh(c, m - 1)
                    if m == 2 and not first:
                        turn_out(c - 1)
            over_chunks(chunk)(pe)
            weigh(NCH - 1, NT - 1)
            denominators(NCH - 1)
            pe.wait_ge(attended_done, NCH)
            turn_out(NCH - 1)


def kernel(x, adj, L0_gnn_Wq, L0_gnn_Wk, L0_gnn_Wv, L0_gnn_weightr, L0_gnn_weightd, L0_gnn_bias,
           L1_gnn_weight, L1_gnn_weight_a1, L1_gnn_weight_a2):
    import numpy as np
    import concourse.bacc as bacc
    from concourse.bass_utils import run_bass_kernel_spmd

    arrays = dict(
        x=np.ascontiguousarray(x), adj=np.ascontiguousarray(adj),
        wq=np.ascontiguousarray(L0_gnn_Wq), wk=np.ascontiguousarray(L0_gnn_Wk),
        wv=np.ascontiguousarray(L0_gnn_Wv),
        wo=np.stack([np.asarray(L0_gnn_weightr), np.asarray(L0_gnn_weightd)]),
        bias=np.ascontiguousarray(L0_gnn_bias), w1=np.ascontiguousarray(L1_gnn_weight),
        a12=np.concatenate([np.asarray(L1_gnn_weight_a1), np.asarray(L1_gnn_weight_a2)], axis=1))
    nc = bacc.Bacc("TRN2", target_bir_lowering=False, num_devices=1)
    args = [nc.dram_tensor(n, a.shape, mybir.dt.from_np(a.dtype), kind="ExternalInput").ap()
            for n, a in arrays.items()]
    out = nc.dram_tensor("out", (N, D), F32, kind="ExternalOutput").ap()
    build(nc, *args, out)
    r = run_bass_kernel_spmd(nc, [arrays], core_ids=[0])
    return r.results[0]["out"]
```

```python
from contextlib import ExitStack

import concourse.bass as bass
from concourse import mybir
from concourse.alu_op_type import AluOpType as ALU

F32 = mybir.dt.float32
F32R = mybir.dt.float32r
BF16 = mybir.dt.bfloat16
I32 = mybir.dt.int32
ACT = mybir.ActivationFunctionType
AX = mybir.AxisListType

P = 128
N = 4096
D = 128
HEADS = 2
DH = D // HEADS
CH = 512
NCH = N // CH
NT = N // P
TPC = CH // P
GROUPS = N // CH
UNITS = TPC * GROUPS
WIDE = 2 * CH
WIDES = N // WIDE
STAGES = 4
EPS = 1e-5
MASKED = -float(2 ** 53)
SCALE = float(DH) ** -0.5
FACTOR_STEPS = 5
SLOPE0 = 0.01
SLOPE1 = 0.2
LOWEST = -3.0e38

FIRST_UNIT, LAST_UNIT = 4, 29
TURN = LAST_UNIT + 2
FIRST_TOP, LAST_TOP = 3, 25
AHEAD = 3


def spread(count, first, last, m):
    return [v for v in range(count) if first + v * (last - first + 1) // count == m]


def halves_at(m):
    return spread(HEADS * UNITS, FIRST_UNIT, LAST_UNIT, m)


def tops_at(m):
    return spread(TPC * WIDES, FIRST_TOP, LAST_TOP, m)


def need(engine, semaphore, value):
    if not isinstance(value, int) or value > 0:
        engine.wait_ge(semaphore, value)


def over_chunks(body):
    def run(engine):
        body(0, 0)
        with engine.Fori(0, (NCH - 2) // 2) as i:
            body(i * 2 + 1, 1)
            body(i * 2 + 2, 0)
        body(NCH - 1, (NCH - 1) % 2)
    return run


def build(nc, x, adj, wq, wk, wv, wo, bias, w1, a12, out):
    q_dram = nc.dram_tensor("q_scaled", (D, N), F32, kind="Internal").ap()
    f1_dram = nc.dram_tensor("f1", (NT, P), F32, kind="Internal").ap()
    x1_dram = nc.dram_tensor("x1", (P, NT, D), F32, kind="Internal").ap()
    mask_dram = nc.dram_tensor("mask", (NCH, P, TPC, N), BF16, kind="Internal").ap()
    with ExitStack() as keep:
        def sb(name, shape, dt, ctx=keep):
            return ctx.enter_context(nc.sbuf_tensor(name, shape, dt))

        shared = dict(
            values=sb("values", [P, NT, D], F32),
            mask=sb("mask_sb", [P, 2, TPC, N], BF16),
            ident=sb("ident", [P, P], F32),
            ident16=sb("ident16", [P, P], BF16),
            ident_r=sb("ident_r", [P, P], F32R),
            ones=sb("ones", [P, P], F32),
            stats=sb("stats", [P, NT, 6], F32),
            moments=sb("moments", [P, NT, 2], F32),
            rstd=sb("rstd", [P, NT], F32),
            std=sb("std", [P, NT], F32),
            newton=sb("newton", [P, NT], F32),
            probs=sb("probs", [P, 2, HEADS, CH], F32),
        )
        shared["nodes_ready"] = keep.enter_context(nc.semaphore("nodes_ready"))
        with ExitStack() as ctx:
            layer0(nc, ctx, shared, x, adj, wq, wk, wv, wo, bias, q_dram, mask_dram, x1_dram)
        with ExitStack() as ctx:
            layer1(nc, ctx, shared, w1, a12, mask_dram, x1_dram, f1_dram, out)


def aggregate(nc, T, tiles):
    for t in tiles:
        last = nc.vector.bn_aggr(T["moments"][:, t, :], T["stats"][:, t, :])
    return last


def norm_factors(nc, dve, T, tiles, part, chain, sqrt_done, var_ready):
    some = slice(tiles[0], tiles[-1] + 1)
    nc.vector.tensor_scalar(T["newton"][:, some], T["moments"][:, some, 1], EPS, None,
                            ALU.add).then_inc(var_ready, 1)
    dve.wait_ge(sqrt_done, part + 1)
    rstd, std, newton = T["rstd"][:, some], T["std"][:, some], T["newton"][:, some]
    chain(nc.vector.reciprocal(rstd, std))
    chain(nc.vector.tensor_tensor(std, rstd, rstd, ALU.mult))
    chain(nc.vector.tensor_tensor(std, std, newton, ALU.mult))
    chain(nc.vector.tensor_scalar(std, std, -0.5, 1.5, ALU.mult, ALU.add))
    chain(nc.vector.tensor_tensor(rstd, rstd, std, ALU.mult))


def chained(dve, semaphore):
    count = [0]

    def chain(instruction):
        count[0] += 1
        instruction.then_inc(semaphore, 1)
        dve.wait_ge(semaphore, count[0])
    return chain


def layer0(nc, ctx, T, x, adj, wq, wk, wv, wo, bias, q_dram, mask_dram, x1_dram):
    def sb(name, shape, dt):
        return ctx.enter_context(nc.sbuf_tensor(name, shape, dt))

    def sem(name):
        return ctx.enter_context(nc.semaphore("l0_" + name))

    values, mask, probs = T["values"], T["mask"], T["probs"]
    ident, ident16, ident_r, ones = T["ident"], T["ident16"], T["ident_r"], T["ones"]
    spare = mask[:, 1].rearrange("p t m -> p (t m)").bitcast(F32)
    nodes = spare[:, 0:NT * D].rearrange("p (t d) -> p t d", d=D)
    centred = spare[:, NT * D:NT * D + 2 * CH].rearrange("p (b n) -> p b n", b=2)
    ht = spare[:, NT * D + 2 * CH:NT * D + 4 * CH].rearrange("p (b n) -> p b n", b=2)
    k_split = [sb(f"k_split{h}", [P, N], F32R) for h in range(HEADS)]
    k_one = [sb(f"k_one{h}", [DH + 1, N], F32R) for h in range(HEADS)]
    q_high = [sb(f"q_high{h}", [P, 2, CH], F32R) for h in range(HEADS)]
    q_low = [sb(f"q_low{h}", [DH + 1, 2, CH], F32R) for h in range(HEADS)]
    q_raw = sb("q_raw", [P, HEADS, CH], F32)
    sums = sb("sums", [P, HEADS, CH], F32)
    staged = sb("staged", [P, STAGES, CH], I32)
    row_max = sb("row_max", [P, HEADS, TPC, GROUPS], F32)
    pause = sb("pause", [P, 1], F32)
    top = sb("top", [P, HEADS * TPC], F32)
    neg_max = sb("neg_max", [P, HEADS * TPC, DH + 1], F32R)
    w_k = sb("w_k", [P, HEADS, 2 * DH], F32)
    w_q = sb("w_q", [P, D], F32)
    w_v = sb("w_v", [P, D], F32)
    w_now = sb("w_now", [P, D], F32)
    bias_all = sb("bias_all", [P, D], F32)
    y = sb("y", [P, CH], F32)
    y_act = sb("y_act", [P, CH], F32)
    attended = sb("attended", [P, CH], F32)
    rden = sb("rden", [P, HEADS * TPC], F32)
    x_rows = sb("x_rows", [P, CH], F32)
    row_stats = sb("row_stats", [P, TPC, 6], F32)
    nodes1 = mask[:, 0].rearrange("p t m -> p (t m)").bitcast(F32)[:, 0:NT * D]

    scores = [ctx.enter_context(nc.psum_tensor(f"scores{b}", [P, HEADS, CH], F32)) for b in range(2)]
    rough = ctx.enter_context(nc.psum_tensor("rough", [P, HEADS, CH], F32))
    weighted = ctx.enter_context(nc.psum_tensor("weighted", [P, CH], F32))
    misc = ctx.enter_context(nc.psum_tensor("misc", [P, CH], F32))

    rough_banks = [rough[:, 0, :], rough[:, 1, :], misc[:]]
    ps_t = weighted
    ps_k = [scores[0][:, 0, :], scores[0][:, 1, :]]
    ps_q, ps_v = scores[1][:, 0, :], scores[1][:, 1, :]

    x_loaded = [sem(f"x_loaded{k}") for k in range(NCH)]
    w_loaded, b_loaded = sem("w_loaded"), sem("b_loaded")
    ident_made, consts = sem("ident"), sem("consts")
    stats_done, var_ready, sqrt_done, norm_chain = sem("stats"), sem("var"), sem("sqrt"), sem("chain")
    centred_ready, turned, ht_ready = sem("centred"), sem("turned"), sem("ht")
    projected, k_high_done, k_done, q_done, v_done = (
        sem("projected"), sem("k_high"), sem("k"), sem("q"), sem("v"))
    q_stored, q_raw_loaded = sem("q_stored"), sem("q_raw")
    q_high_done, q_low_done = sem("q_high"), sem("q_low")
    adj_loaded = [sem(f"adj{s}") for s in range(STAGES)]
    mask_done, mask_stored = sem("mask"), sem("mask_stored")
    pool_converted, dve_converted = sem("pool_converted"), sem("dve_converted")
    rough_done, rough_read = sem("rough"), sem("rough_read")
    max_done, max_turned, max_row = sem("max"), sem("max_turned"), sem("max_row")
    scores_done, exp_done, pv_done = sem("scores"), sem("exp"), sem("pv")
    sum_done = [sem("sum0"), sem("sum1")]
    den_done, epilogue, out_done = sem("den"), sem("epilogue"), sem("out")
    attended_done, k_one_done = sem("attended"), sem("k_one")
    stats1_done = sem("stats1")
    x_rows_loaded, x1_stored = sem("x_rows"), sem("x1_stored")

    x_t = x.rearrange("(c p) d -> p c d", p=P)
    adj_t = adj.rearrange("(c p) m -> c p m", p=P)
    NORM_PARTS = [range(2 * TPC), range(2 * TPC, NT)]
    LAG = 2
    PER_GROUP = TPC * HEADS
    NEPI = 5

    with nc.Block() as block:
        @block.sync
        def _(sp):
            for k in range(NCH):
                sp.dma_start(nodes[:, k * TPC:(k + 1) * TPC, :],
                             x_t[:, k * TPC:(k + 1) * TPC, :]).then_inc(x_loaded[k], 16)
            sp.dma_start(bias_all[:], bias.partition_broadcast(P)).then_inc(b_loaded, 16)

            def load_adjacency(c, units=range(UNITS)):
                for u in units:
                    g, j = u // TPC, u % TPC
                    if not (isinstance(c, int) and c == 0):
                        sp.wait_ge(mask_done, c * UNITS + (u - STAGES + 1))
                    elif j < TPC - 1:
                        need(sp, pool_converted, (g - 1) * (TPC - 1) + (j + 1))
                    else:
                        need(sp, dve_converted, g)
                    rows = adj_t[bass.ds(c * TPC + j, 1), :, g * CH:(g + 1) * CH]
                    sp.dma_start(staged[:, u % STAGES, :],
                                 rows.rearrange("o p m -> (o p) m")).then_inc(adj_loaded[u % STAGES], 16)

            def load_q(c):
                need(sp, q_low_done, c * HEADS)
                for h in range(HEADS):
                    for twice in range(2):
                        sp.dma_start(q_raw[twice * DH:(twice + 1) * DH, h, :],
                                     q_dram[h * DH:(h + 1) * DH, bass.ts(c, CH)]).then_inc(q_raw_loaded, 16)

            load_adjacency(0, range(2 * STAGES))
            sp.wait_ge(q_stored, 16)
            load_q(0)
            load_adjacency(0, range(2 * STAGES, UNITS))
            sp.wait_ge(q_stored, 16 * NCH)

            def chunk(c, par):
                more = not isinstance(c, int) or c + 1 < NCH
                if more:
                    load_q(c + 1)
                sp.wait_ge(mask_done, (c + 1) * UNITS)
                sp.dma_start(mask_dram[bass.ds(c, 1)].rearrange("o p t m -> (o p) t m"),
                             mask[:, par]).then_inc(mask_stored, 16)
                if more:
                    load_adjacency(c + 1)
                else:
                    sp.wait_ge(scores_done, c * NT)
                    sp.wait_ge(x1_stored, (NCH - 2) * 16)
                    before = (NCH - 2) * CH
                    sp.dma_start(nodes1[:, 0:before], x1_dram.rearrange("p t d -> p (t d)")[:, 0:before]
                                 ).then_inc(T["nodes_ready"], 16)
                if not isinstance(c, int) or c > 0:
                    store_x1(c - 1)
                load_x(c)

            def store_x1(e):
                sp.wait_ge(epilogue, (e + 2) * NEPI)
                sp.dma_start(x1_dram[:, bass.ds(e * TPC, TPC), :],
                             y[:].rearrange("p (t d) -> p t d", t=TPC)).then_inc(x1_stored, 16)
                if isinstance(e, int) and e >= NCH - 2:
                    sp.dma_start(nodes1[:, e * CH:(e + 1) * CH], y[:]).then_inc(T["nodes_ready"], 16)

            def load_x(e):
                need(sp, x1_stored, e * 16)
                sp.dma_start(x_rows[:].rearrange("p (t d) -> p t d", t=TPC),
                             x_t[:, bass.ds(e * TPC, TPC), :]).then_inc(x_rows_loaded, 16)
                sp.dma_start(w_now[:], wo[bass.ds(e // (NCH // 2), 1)]
                             .rearrange("o d e -> (o d) e")).then_inc(x_rows_loaded, 16)
            over_chunks(chunk)(sp)
            store_x1(NCH - 1)
            sp.wait_ge(x1_stored, 16 * NCH)
            sp.wait_ge(mask_stored, 16 * NCH)

        @block.gpsimd
        def _(pool):
            nc.gpsimd.memset(ident[:], 0.0).then_inc(ident_made, 1)
            pool.wait_ge(ident_made, 1)
            nc.gpsimd.affine_select(out=ident[:], in_=ident[:], compare_op=ALU.not_equal, fill=1.0,
                                    base=0, pattern=[[-1, P]], channel_multiplier=1).then_inc(ident_made, 1)
            pool.wait_ge(ident_made, 2)
            nc.gpsimd.tensor_copy(ident16[:], ident[:]).then_inc(ident_made, 1)
            pool.wait_ge(ident_made, 3)
            nc.gpsimd.tensor_copy(ident_r[:], ident[:]).then_inc(ident_made, 1)
            pool.wait_ge(ident_made, 4)
            for h in range(HEADS):
                nc.gpsimd.memset(k_one[h][DH:DH + 1, :].bitcast(F32), 1.0).then_inc(ident_made, 1)
                pool.wait_ge(ident_made, 5 + h)
            for g in range(GROUPS):
                for j in range(TPC - 1):
                    pool.wait_ge(adj_loaded[j], (g + 1) * 16)
                    need(pool, pool_converted, g * (TPC - 1) + j)
                    nc.gpsimd.tensor_scalar(mask[:, 0, j, g * CH:(g + 1) * CH], staged[:, j, :],
                                            0.0, MASKED, ALU.is_le, ALU.mult).then_inc(pool_converted, 1)
            pool.wait_ge(pool_converted, GROUPS * (TPC - 1))

            def chunk(c, par):
                for m in range(NT):
                    pool.wait_ge(exp_done, c * NT + (m + 1))
                    if m == 0:
                        need(pool, den_done, c)
                        nc.gpsimd.tensor_tensor(sums[:, 0, :], probs[:, 0, 0, :],
                                                ones[:, 0:1].broadcast_to([P, CH]), ALU.mult).then_inc(sum_done[0], 1)
                    else:
                        pool.wait_ge(sum_done[0], c * NT + m)
                        nc.gpsimd.tensor_tensor(sums[:, 0, :], sums[:, 0, :], probs[:, m % 2, 0, :],
                                                ALU.add).then_inc(sum_done[0], 1)
            over_chunks(chunk)(pool)

        @block.scalar
        def _(act):
            def round_q(c, par):
                act.wait_ge(q_raw_loaded, (c + 1) * 64)
                for h in range(HEADS):
                    nc.scalar.activation(q_high[h][:, par, :], q_raw[:, h, :],
                                         ACT.Copy).then_inc(q_high_done, 1)

            for h in range(HEADS):
                for twice in range(2):
                    act.dma_start(w_k[:, h, twice * DH:(twice + 1) * DH],
                                  wk[:, h * DH:(h + 1) * DH]).then_inc(w_loaded, 16)
            act.dma_start(w_q[:], wq).then_inc(w_loaded, 16)
            act.dma_start(w_v[:], wv).then_inc(w_loaded, 16)
            def root(part):
                tiles = NORM_PARTS[part]
                some = slice(tiles[0], tiles[-1] + 1)
                act.wait_ge(var_ready, part + 1)
                nc.scalar.activation(T["std"][:, some], T["newton"][:, some], ACT.Sqrt).then_inc(sqrt_done, 1)

            def relu_turned(k):
                act.wait_ge(turned, k + 1)
                need(act, projected, 4 * (k - 1))
                nc.scalar.activation(ht[:, k % 2, :], ps_t[:], ACT.Relu).then_inc(ht_ready, 1)

            root(0)
            relu_turned(0)
            for k in range(NCH):
                cols = slice(k * CH, (k + 1) * CH)
                for h in range(HEADS):
                    act.wait_ge(projected, 4 * k + h + 1)
                    nc.scalar.activation(k_split[h][:, cols], ps_k[h], ACT.Copy).then_inc(k_high_done, 1)
                    nc.scalar.activation(k_one[h][0:DH, cols], ps_k[h][0:DH, :],
                                         ACT.Copy).then_inc(k_one_done, 1)
                if k == 0:
                    root(1)
                act.wait_ge(projected, 4 * k + 3)
                need(act, q_stored, 16 * k)
                nc.scalar.activation(y[:], ps_q, ACT.Copy, scale=SCALE).then_inc(q_done, 1)
                act.wait_ge(q_done, k + 1)
                act.dma_start(q_dram[:, cols], y[:]).then_inc(q_stored, 16)
                if k + 1 < NCH:
                    relu_turned(k + 1)
                act.wait_ge(projected, 4 * k + 4)
                nc.scalar.activation(values[:, k * TPC:(k + 1) * TPC, :].rearrange("p t d -> p (t d)"),
                                     ps_v, ACT.Copy).then_inc(v_done, 1)
                if k == 1:
                    round_q(0, 0)

            def max_rows(c, par):
                act.wait_ge(max_turned, c + 1)
                for h in range(HEADS):
                    nc.scalar.activation(q_low[h][DH:DH + 1, par, :], rough[DH:DH + 1, h, :],
                                         ACT.Copy).then_inc(max_row, 1)

            max_rows(0, 0)

            def chunk(c, par):
                first = isinstance(c, int) and c == 0
                more = not isinstance(c, int) or c + 1 < NCH
                for m in range(NT):
                    s = c * NT + m
                    act.wait_ge(scores_done, s + 1)
                    need(act, pv_done, s - 1)
                    need(act, sum_done[0], s - 1)
                    need(act, sum_done[1], s - 1)
                    nc.scalar.activation(probs[:, m % 2], scores[m % 2][:], ACT.Exp).then_inc(exp_done, 1)
                    if m == 0 and not first:
                        act.wait_ge(pv_done, c * NT)
                        nc.scalar.activation(attended[:], weighted[:], ACT.Copy).then_inc(attended_done, 1)
                    if more and m == 1:
                        round_q(c + 1, 1 - par)
                    if more and m == TURN:
                        max_rows(c + 1, 1 - par)
            over_chunks(chunk)(act)
            act.wait_ge(pv_done, NCH * NT)
            nc.scalar.activation(attended[:], weighted[:], ACT.Copy).then_inc(attended_done, 1)

        @block.vector
        def _(dve):
            chain = chained(dve, norm_chain)
            nc.vector.memset(ones[:], 1.0).then_inc(consts, 1)
            nc.vector.memset(neg_max[:].bitcast(F32), 0.0).then_inc(consts, 1)

            def norm(part):
                tiles = NORM_PARTS[part]
                for t in tiles:
                    if t % TPC == 0:
                        dve.wait_ge(x_loaded[t // TPC], 16)
                    last = nc.vector.bn_stats(T["stats"][:, t, :], nodes[:, t, :])
                last.then_inc(stats_done, 1)
                dve.wait_ge(stats_done, 2 * part + 1)
                aggregate(nc, T, tiles).then_inc(stats_done, 1)
                dve.wait_ge(stats_done, 2 * part + 2)
                norm_factors(nc, dve, T, tiles, part, chain, sqrt_done, var_ready)

            def centre(k):
                need(dve, turned, k - 1)
                for j in range(TPC):
                    t = k * TPC + j
                    last = nc.vector.tensor_scalar(centred[:, k % 2, j * P:(j + 1) * P], nodes[:, t, :],
                                                   T["moments"][:, t, 0:1], T["rstd"][:, t:t + 1],
                                                   ALU.subtract, ALU.mult)
                last.then_inc(centred_ready, 1)

            def convert(c, par, u):
                g, j = u // TPC, u % TPC
                dve.wait_ge(adj_loaded[u % STAGES], (c * GROUPS + (g + 1)) * 16)
                nc.vector.tensor_scalar(mask[:, par, j, g * CH:(g + 1) * CH], staged[:, u % STAGES, :],
                                        0.0, MASKED, ALU.is_le, ALU.mult).then_inc(mask_done, 1)

            def tops(c, par, halves, m):
                summed = m == 0
                for v in halves:
                    u, h = v // HEADS, v % HEADS
                    g, j = u // TPC, u % TPC
                    if h == 0:
                        dve.wait_ge(mask_done, c * UNITS + (u + 1))
                    dve.wait_ge(rough_done, c * UNITS * HEADS + (v + 1))
                    if h == 0 and u + 1 < UNITS:
                        convert(c, par, u + 1)
                    elif not summed:
                        sum_head1(c - 1, m - 1)
                        summed = True
                    else:
                        nc.vector.memset(pause[:], 0.0)
                    bank = rough_banks[v % 3]
                    nc.vector.tensor_tensor_reduce(
                        out=bank, in0=bank, in1=mask[:, par, j, g * CH:(g + 1) * CH],
                        scale=1.0, scalar=LOWEST, op0=ALU.add, op1=ALU.max,
                        accum_out=row_max[:, h, j, g:g + 1]).then_inc(rough_read, 1)
                if not summed:
                    sum_head1(c - 1, m - 1)

            def maxima(c):
                dve.wait_ge(rough_read, (c + 1) * UNITS * HEADS)
                nc.vector.tensor_reduce(top[:], row_max[:].rearrange("p h j g -> p (h j) g"), AX.X,
                                        ALU.max).then_inc(max_done, 1)
                dve.wait_ge(max_done, c * 2 + 1)
                nc.vector.tensor_scalar(neg_max[:, :, DH], top[:], -1.0, None,
                                        ALU.mult).then_inc(max_done, 1)

            def lower_q(c, par):
                for h in range(HEADS):
                    dve.wait_ge(q_high_done, c * HEADS + (h + 1))
                    nc.vector.tensor_tensor(q_low[h][0:DH, par, :], q_raw[0:DH, h, :],
                                            q_high[h][0:DH, par, :].bitcast(F32),
                                            ALU.subtract).then_inc(q_low_done, 1)

            def convert_first(g):
                j = TPC - 1
                dve.wait_ge(adj_loaded[j], (g + 1) * 16)
                nc.vector.tensor_scalar(mask[:, 0, j, g * CH:(g + 1) * CH], staged[:, j, :],
                                        0.0, MASKED, ALU.is_le, ALU.mult).then_inc(dve_converted, 1)

            def top_first(v):
                u, h = v // HEADS, v % HEADS
                g, j = u // TPC, u % TPC
                if j < TPC - 1:
                    dve.wait_ge(pool_converted, g * (TPC - 1) + (j + 1))
                else:
                    dve.wait_ge(dve_converted, g + 1)
                dve.wait_ge(rough_done, v + 1)
                bank = rough_banks[v % 3]
                nc.vector.tensor_tensor_reduce(
                    out=bank, in0=bank, in1=mask[:, 0, j, g * CH:(g + 1) * CH],
                    scale=1.0, scalar=LOWEST, op0=ALU.add, op1=ALU.max,
                    accum_out=row_max[:, h, j, g:g + 1]).then_inc(rough_read, 1)

            norm(0)
            centre(0)
            centre(1)
            norm(1)
            for k in range(NCH + LAG):
                halves = list(range(max(k - LAG, 0) * PER_GROUP, max(k - LAG + 1, 0) * PER_GROUP))
                for v in halves[:2]:
                    top_first(v)
                for h in range(HEADS):
                    if k < NCH:
                        cols = slice(k * CH, (k + 1) * CH)
                        dve.wait_ge(k_high_done, HEADS * k + h + 1)
                        nc.vector.tensor_tensor(k_split[h][DH:P, cols], ps_k[h][DH:P, :],
                                                k_split[h][DH:P, cols].bitcast(F32),
                                                ALU.subtract).then_inc(k_done, 1)
                    for v in halves[2 + 2 * h:4 + 2 * h]:
                        top_first(v)
                if k + 2 < NCH:
                    centre(k + 2)
                if k < GROUPS:
                    convert_first(k)
                for v in halves[6:]:
                    top_first(v)
                if k == 1:
                    lower_q(0, 0)
            dve.wait_ge(pool_converted, GROUPS * (TPC - 1))
            dve.wait_ge(dve_converted, GROUPS)
            nc.vector.memset(pause[:], 0.0).then_inc(mask_done, UNITS)
            dve.wait_ge(consts, 2)
            maxima(0)
            nc.vector.memset(y_act[:], 0.0).then_inc(epilogue, NEPI)

            def sum_head1(c, m):
                dve.wait_ge(exp_done, c * NT + (m + 1))
                if m == 0:
                    need(dve, den_done, c)
                    nc.vector.tensor_copy(sums[:, 1, :], probs[:, 0, 1, :]).then_inc(sum_done[1], 1)
                else:
                    dve.wait_ge(sum_done[1], c * NT + m)
                    nc.vector.tensor_tensor(sums[:, 1, :], sums[:, 1, :], probs[:, m % 2, 1, :],
                                            ALU.add).then_inc(sum_done[1], 1)

            def finish(e):
                before = (e + 1) * NEPI
                dve.wait_ge(den_done, e + 1)
                nc.vector.reciprocal(rden[:], misc[:, 0:HEADS * TPC]).then_inc(epilogue, 1)
                dve.wait_ge(x_rows_loaded, (e + 1) * 32)
                dve.wait_ge(out_done, e + 1)
                dve.wait_ge(epilogue, before + 1)
                for h in range(HEADS):
                    for j in range(TPC):
                        cols = slice(j * P, (j + 1) * P)
                        last = nc.vector.scalar_tensor_tensor(
                            y[:, cols], rough[:, h, cols], rden[:, h * TPC + j:h * TPC + j + 1],
                            y[:, cols] if h else bias_all[:], ALU.mult, ALU.add)
                    last.then_inc(epilogue, 1)
                    dve.wait_ge(epilogue, before + (2 + h))
                nc.vector.scalar_tensor_tensor(y_act[:], y[:], SLOPE0, y[:], ALU.mult,
                                               ALU.max).then_inc(epilogue, 1)
                dve.wait_ge(epilogue, before + 4)
                nc.vector.tensor_tensor(y[:], x_rows[:], y_act[:], ALU.add).then_inc(epilogue, 1)
                dve.wait_ge(epilogue, before + NEPI)
                for j in range(TPC):
                    last = nc.vector.bn_stats(row_stats[:, j, :], y[:, j * P:(j + 1) * P])
                last.then_inc(stats1_done, 1)
                dve.wait_ge(stats1_done, 2 * e + 1)
                nc.vector.tensor_scalar(T["stats"][:, bass.ds(e * TPC, TPC), :], row_stats[:], 1.0, None,
                                        ALU.mult).then_inc(stats1_done, 1)

            def chunk(c, par):
                first = isinstance(c, int) and c == 0
                more = not isinstance(c, int) or c + 1 < NCH
                for m in range(NT):
                    halves = halves_at(m) if more else []
                    if m > 0 and not halves:
                        sum_head1(c, m - 1)
                    if m == 2 and not first:
                        finish(c - 1)
                    if m == 3 and more:
                        need(dve, scores_done, c * NT)
                        lower_q(c + 1, 1 - par)
                    if more:
                        if m == FIRST_UNIT:
                            need(dve, mask_stored, c * 16)
                            convert(c + 1, 1 - par, 0)
                        if halves:
                            tops(c + 1, 1 - par, halves, m)
                        if m == LAST_UNIT + 1:
                            maxima(c + 1)
                    elif m == 8:
                        dve.wait_ge(stats1_done, 2 * (NCH - 1))
                        aggregate(nc, T, range(NT - TPC))
                sum_head1(c, NT - 1)
            over_chunks(chunk)(dve)
            finish(NCH - 1)

        @block.tensor
        def _(pe):
            pe.wait_ge(ident_made, 6)
            pe.wait_ge(consts, 2)
            pe.wait_ge(w_loaded, 16 * 6)
            pe.wait_ge(b_loaded, 16)

            def turn(k):
                pe.wait_ge(centred_ready, k + 1)
                need(pe, ht_ready, k)
                for j in range(TPC):
                    cols = slice(j * P, (j + 1) * P)
                    last = nc.tensor.transpose(ps_t[:, cols], centred[:, k % 2, cols], ident[:])
                last.then_inc(turned, 1)

            def rough_scores(c, par, v):
                u, h = v // HEADS, v % HEADS
                g, j = u // TPC, u % TPC
                if v >= 3:
                    pe.wait_ge(rough_read, c * UNITS * HEADS + (v - 2))
                nc.tensor.matmul(rough_banks[v % 3], q_high[h][:, par, j * P:(j + 1) * P],
                                 k_split[h][:, g * CH:(g + 1) * CH], start=True,
                                 stop=True).then_inc(rough_done, 1)

            def turn_maxima(c):
                pe.wait_ge(max_done, (c + 1) * 2)
                for h in range(HEADS):
                    for j in range(TPC):
                        last = nc.tensor.matmul(rough[0:DH + 1, h, j * P:(j + 1) * P],
                                                neg_max[:, h * TPC + j, :], ident_r[:], start=True,
                                                stop=True)
                last.then_inc(max_turned, 1)

            turn(0)
            for k in range(NCH + LAG):
                halves = list(range(max(k - LAG, 0) * PER_GROUP, max(k - LAG + 1, 0) * PER_GROUP))
                if k == LAG:
                    pe.wait_ge(q_high_done, HEADS)
                if k == NCH:
                    pe.wait_ge(k_done, HEADS * NCH)
                for v in halves[:2]:
                    rough_scores(0, 0, v)
                if k < NCH:
                    pe.wait_ge(ht_ready, k + 1)
                for h in range(HEADS):
                    if k < NCH:
                        need(pe, k_done, HEADS * (k - 1) + h + 1)
                        need(pe, k_one_done, HEADS * (k - 1) + h + 1)
                        nc.tensor.matmul(ps_k[h], w_k[:, h, :], ht[:, k % 2, :], start=True,
                                         stop=True).then_inc(projected, 1)
                    for v in halves[2 + h:3 + h]:
                        rough_scores(0, 0, v)
                if k + 1 < NCH:
                    turn(k + 1)
                for v in halves[4:5]:
                    rough_scores(0, 0, v)
                if k < NCH:
                    need(pe, q_done, k)
                    nc.tensor.matmul(ps_q, w_q[:], ht[:, k % 2, :], start=True, stop=True).then_inc(projected, 1)
                for v in halves[5:6]:
                    rough_scores(0, 0, v)
                if k < NCH:
                    need(pe, v_done, k)
                    for j in range(TPC):
                        cols = slice(j * P, (j + 1) * P)
                        last = nc.tensor.matmul(ps_v[:, cols], ht[:, k % 2, cols], w_v[:], start=True, stop=True)
                    last.then_inc(projected, 1)
                for v in halves[6:]:
                    rough_scores(0, 0, v)
            pe.wait_ge(k_one_done, HEADS * NCH)
            pe.wait_ge(v_done, NCH)
            turn_maxima(0)

            def score(c, par, m):
                s = c * NT + m
                keys = slice(m * P, (m + 1) * P)
                bank = scores[m % 2]
                if m == 0:
                    pe.wait_ge(q_high_done, (c + 1) * HEADS)
                need(pe, exp_done, s - 1)
                for h in range(HEADS):
                    nc.tensor.matmul(bank[:, h, :], k_split[h][:, keys], q_high[h][:, par, :],
                                     start=True, stop=False)
                if m == 0:
                    pe.wait_ge(mask_done, (c + 1) * UNITS)
                for j in range(TPC):
                    for h in range(HEADS):
                        nc.tensor.matmul(bank[:, h, j * P:(j + 1) * P], mask[:, par, j, keys], ident16[:],
                                         start=False, stop=False)
                if m == 0:
                    pe.wait_ge(q_low_done, (c + 1) * HEADS)
                    pe.wait_ge(max_row, (c + 1) * HEADS)
                for h in range(HEADS):
                    last = nc.tensor.matmul(bank[:, h, :], k_one[h][:, keys], q_low[h][:, par, :],
                                            start=False, stop=True)
                last.then_inc(scores_done, 1)

            def weigh(c, m):
                pe.wait_ge(exp_done, c * NT + (m + 1))
                for h in range(HEADS):
                    last = nc.tensor.matmul(weighted[h * DH:(h + 1) * DH, :],
                                            values[:, m, h * DH:(h + 1) * DH], probs[:, m % 2, h, :],
                                            start=(m == 0), stop=(m == NT - 1))
                last.then_inc(pv_done, 1)

            def denominators(e):
                pe.wait_ge(sum_done[0], (e + 1) * NT)
                pe.wait_ge(sum_done[1], (e + 1) * NT)
                pe.wait_ge(epilogue, (e + 1) * NEPI)
                for h in range(HEADS):
                    for j in range(TPC):
                        o = h * TPC + j
                        last = nc.tensor.matmul(misc[:, o:o + 1], sums[:, h, j * P:(j + 1) * P],
                                                ones[:, 0:1], start=True, stop=True)
                last.then_inc(den_done, 1)

            def project(e):
                pe.wait_ge(x_rows_loaded, (e + 1) * 32)
                for h in range(HEADS):
                    dims = slice(h * DH, (h + 1) * DH)
                    for j in range(TPC):
                        cols = slice(j * P, (j + 1) * P)
                        last = nc.tensor.matmul(rough[:, h, cols], attended[dims, cols],
                                                w_now[dims, :], start=True, stop=True)
                last.then_inc(out_done, 1)

            def chunk(c, par):
                first = isinstance(c, int) and c == 0
                more = not isinstance(c, int) or c + 1 < NCH
                for m in range(NT):
                    score(c, par, m)
                    if more:
                        if m == FIRST_UNIT:
                            pe.wait_ge(q_high_done, (c + 2) * HEADS)
                            if not first:
                                pe.wait_ge(epilogue, (c + 1) * NEPI)
                        if m == TURN:
                            turn_maxima(c + 1)
                        for v in halves_at(m)[:1]:
                            rough_scores(c + 1, 1 - par, v)
                    if m == 0 and not first:
                        weigh(c - 1, NT - 1)
                    if m == 1 and not first:
                        denominators(c - 1)
                        pe.wait_ge(attended_done, c)
                        project(c - 1)
                    if m > 0:
                        weigh(c, m - 1)
                    if more:
                        for v in halves_at(m)[1:]:
                            rough_scores(c + 1, 1 - par, v)
            over_chunks(chunk)(pe)
            weigh(NCH - 1, NT - 1)
            denominators(NCH - 1)
            pe.wait_ge(attended_done, NCH)
            project(NCH - 1)


def layer1(nc, ctx, T, w1, a12, mask_dram, x1_dram, f1_dram, out):
    def sb(name, shape, dt):
        return ctx.enter_context(nc.sbuf_tensor(name, shape, dt))

    def sem(name):
        return ctx.enter_context(nc.semaphore("l1_" + name))

    values, mask = T["values"], T["mask"]
    ident, ident16, ident_r, ones = T["ident"], T["ident16"], T["ident_r"], T["ones"]
    nodes = mask[:, 0].rearrange("p t m -> p (t m)").bitcast(F32)[:, 0:NT * D]
    nodes = nodes.rearrange("p (t d) -> p t d", d=D)
    x1_rows = sb("x1_rows", [P, CH], F32)
    centred = sb("centred", [P, NCH, CH], F32)
    ht = sb("ht", [P, 2, CH], F32)
    RING = 4
    probs = T["probs"][:].rearrange("p a b n -> p (a b) n")
    relu = sb("relu", [P, RING, CH], F32)
    w_hf = sb("w_hf", [P, D + 2], F32)
    w_ht = sb("w_ht", [P, D], F32)
    a_col = sb("a_col", [P, 2], F32)
    w_f2all = sb("w_f2all", [P, P], F32)
    f1_rows = sb("f1_rows", [NT, P], F32)
    f2_all = sb("f2_all", [P, N], F32)
    f1_now = sb("f1_now", [P, 2, CH], F32)
    f_col = sb("f_col", [P, NT, 2], F32)
    f2_relu = sb("f2_relu", [P, NT], F32)
    f2_exp = sb("f2_exp", [P, NT], F32)
    arg = sb("arg", [P, RING, CH], F32)
    junk = sb("junk", [P, 4, WIDE], BF16)
    row_max = sb("row_max1", [P, TPC, WIDES], F32)
    f1_slope = sb("f1_slope", [P, NT], F32)
    tops = sb("tops", [P, 4, TPC], F32)
    shift = sb("shift", [P, TPC, 2], F32R)
    shift_row = sb("shift_row", [P, 2, CH], F32R)
    ones_r = sb("ones_r", [P, P], F32R)
    sums = sb("sums1", [P, CH], F32)
    rden = sb("rden1", [P, TPC], F32)
    attended = sb("attended1", [P, CH], F32)
    result = sb("result", [P, CH], F32)

    scores = [ctx.enter_context(nc.psum_tensor(f"e{b}", [P, CH], F32)) for b in range(RING)]
    weighted = ctx.enter_context(nc.psum_tensor("weighted1", [P, CH], F32))
    misc = ctx.enter_context(nc.psum_tensor("misc1", [P, CH], F32))
    rows = ctx.enter_context(nc.psum_tensor("rows", [P, CH], F32))
    ps_f = ctx.enter_context(nc.psum_tensor("ps_f", [P, CH], F32))
    ps_t = [weighted, misc]
    ps_hf = [[rows, ps_f], [scores[1], scores[2]]]
    ps_hf = [[bank[:, 0:2 * (D + 2)].rearrange("p (t w) -> p t w", w=D + 2) for bank in pair] for pair in ps_hf]
    ps_f2 = [scores[0], scores[3]]

    f1_turned, f1_ready, f1_stored = sem("f1_turned"), sem("f1_ready"), sem("f1_stored")
    f1_loaded = [sem("f1_loaded0"), sem("f1_loaded1")]
    x1_loaded, stored = sem("x1"), sem("stored")
    w_loaded, consts, w_turned, w_copied, w_folded = (
        sem("w_loaded"), sem("consts"), sem("w_turned"), sem("w_copied"), sem("w_folded"))
    stats_done, var_ready, sqrt_done, norm_chain = sem("stats"), sem("var"), sem("sqrt"), sem("chain")
    centred_ready = [sem("centred0"), sem("centred1")]
    turned, ht_ready = sem("turned"), sem("ht")
    projected, h_done, f_done, all_done = sem("projected"), sem("h"), sem("f"), sem("all")
    f_scaled = sem("f_scaled")
    mask_loaded = [[sem(f"mask{par}{j}") for j in range(TPC)] for par in range(2)]
    top_done, shift_done, shift_turned, shift_copied = (
        sem("top"), sem("shift"), sem("shift_turned"), sem("shift_row"))
    scores_done, relu_done, arg_done, exp_done, pv_done, sum_done = (
        sem("scores"), sem("relu"), sem("arg"), sem("exp"), sem("pv"), sem("sum"))
    attended_done = sem("attended")
    den_done, epilogue, out_turned = sem("den"), sem("epilogue"), sem("out_turned")

    def mask_loads(c, par):
        return (c + (2 - par)) // 2 * 16
    NSH = 6
    NEPI = 2
    out_t = out.rearrange("(t p) d -> p t d", p=P)

    with nc.Block() as block:
        @block.sync
        def _(sp):
            sp.dma_start(w_hf[:, 0:D], w1).then_inc(w_loaded, 16)
            sp.dma_start(a_col[:], a12).then_inc(w_loaded, 16)

            def load_mask(c, par):
                need(sp, scores_done, (c - 1) * NT)
                for j in range(TPC):
                    sp.dma_start(mask[:, 1 - par, j, :], mask_dram[bass.ds(c, 1), :, j, :]
                                 .rearrange("o p m -> (o p) m")).then_inc(mask_loaded[par][j], 16)

            def load_f1(c, par):
                need(sp, relu_done, (c - 1) * NT)
                sp.dma_start(f1_now[:, par, :], f1_dram[bass.ds(c * TPC, TPC), :]
                             .rearrange("t p -> (t p)").partition_broadcast(P)).then_inc(f1_loaded[par], 16)

            def store(e):
                sp.wait_ge(epilogue, (e + 2) * NEPI)
                sp.dma_start(out_t[:, bass.ds(e * TPC, TPC), :],
                             result[:].rearrange("p (t d) -> p t d", t=TPC)).then_inc(stored, 16)

            def load_x1(e):
                need(sp, stored, e * 16)
                sp.dma_start(x1_rows[:].rearrange("p (t d) -> p t d", t=TPC),
                             x1_dram[:, bass.ds(e * TPC, TPC), :]).then_inc(x1_loaded, 16)

            load_mask(0, 0)
            sp.wait_ge(f1_ready, 1)
            sp.dma_start(f1_dram, f1_rows[:]).then_inc(f1_stored, 16)
            sp.wait_ge(f1_stored, 16)
            load_f1(0, 0)

            def chunk(c, par):
                first = isinstance(c, int) and c == 0
                more = not isinstance(c, int) or c + 1 < NCH
                if more:
                    if first:
                        for b in range(2):
                            sp.wait_ge(centred_ready[b], NCH // 2)
                    load_mask(c + 1, 1 - par)
                    load_f1(c + 1, 1 - par)
                if not first:
                    store(c - 1)
                load_x1(c)
            over_chunks(chunk)(sp)
            store(NCH - 1)
            sp.wait_ge(stored, 16 * NCH)

        @block.gpsimd
        def _(pool):
            nc.gpsimd.memset(ones_r[:].bitcast(F32), 1.0).then_inc(consts, 1)
            nc.gpsimd.memset(shift_row[:].bitcast(F32), 0.0).then_inc(consts, 1)
            nc.gpsimd.memset(result[:], 0.0).then_inc(epilogue, NEPI)
            pool.wait_ge(T["nodes_ready"], 48)
            pool.wait_ge(norm_chain, FACTOR_STEPS)
            for k in range(1, NCH, 2):
                for j in range(TPC):
                    t = k * TPC + j
                    last = nc.gpsimd.tensor_scalar(centred[:, k, j * P:(j + 1) * P], nodes[:, t, :],
                                                   T["moments"][:, t, 0:1], T["rstd"][:, t:t + 1],
                                                   ALU.subtract, ALU.mult)
                last.then_inc(centred_ready[k % 2], 1)

            def chunk(c, par):
                for m in range(NT):
                    pool.wait_ge(exp_done, c * NT + (m + 1))
                    if m == 0:
                        need(pool, den_done, c)
                        nc.gpsimd.tensor_tensor(sums[:], probs[:, 0, :],
                                                ones[:, 0:1].broadcast_to([P, CH]), ALU.mult).then_inc(sum_done, 1)
                    else:
                        pool.wait_ge(sum_done, c * NT + m)
                        nc.gpsimd.tensor_tensor(sums[:], sums[:], probs[:, m % RING, :],
                                                ALU.add).then_inc(sum_done, 1)
            over_chunks(chunk)(pool)

        @block.scalar
        def _(act):
            act.wait_ge(var_ready, 1)
            nc.scalar.activation(T["std"][:], T["newton"][:], ACT.Sqrt).then_inc(sqrt_done, 1)

            def relu_turned(k):
                act.wait_ge(turned, k + 1)
                need(act, projected, 2 * (k - 1))
                nc.scalar.activation(ht[:, k % 2, :], ps_t[k % 2][:], ACT.Relu).then_inc(ht_ready, 1)

            relu_turned(0)
            for k in range(NCH):
                cols = slice(k * CH, (k + 1) * CH)
                if k + 1 < NCH:
                    relu_turned(k + 1)
                act.wait_ge(projected, 2 * k + 1)
                nc.scalar.activation(f2_all[:, cols], ps_f2[k % 2][:], ACT.Copy).then_inc(all_done, 1)
                act.wait_ge(projected, 2 * k + 2)
                for pair in range(2):
                    tiles = slice(k * TPC + 2 * pair, k * TPC + 2 * pair + 2)
                    last = nc.scalar.activation(values[:, tiles, :], ps_hf[k % 2][pair][:, :, 0:D], ACT.Copy)
                last.then_inc(h_done, 1)

            def copy_shift(c, par):
                act.wait_ge(shift_turned, c + 1)
                nc.scalar.activation(shift_row[0:2, par, :], rows[0:2, :], ACT.Copy).then_inc(shift_copied, 1)

            act.wait_ge(consts, 2)
            act.wait_ge(f_scaled, 3)

            def relu_of(c, par, m):
                if m == 0:
                    act.wait_ge(f1_loaded[par], mask_loads(c, par))
                need(act, arg_done, c * NT + (m - RING + 1))
                nc.scalar.activation(relu[:, m % RING, :], f1_now[:, par, :], ACT.Relu,
                                     bias=f2_relu[:, m:m + 1], scale=1.0 - SLOPE1).then_inc(relu_done, 1)

            def exp_of(c, m):
                s = c * NT + m
                act.wait_ge(arg_done, s + 1)
                need(act, pv_done, s - RING + 1)
                need(act, sum_done, s - RING + 1)
                nc.scalar.activation(probs[:, m % RING, :], arg[:, m % RING, :], ACT.Exp,
                                     bias=f2_exp[:, m:m + 1]).then_inc(exp_done, 1)

            for m in range(AHEAD):
                relu_of(0, 0, m)
            copy_shift(0, 0)

            def chunk(c, par):
                first = isinstance(c, int) and c == 0
                more = not isinstance(c, int) or c + 1 < NCH
                for m in range(NT):
                    if m + AHEAD < NT:
                        relu_of(c, par, m + AHEAD)
                    elif more:
                        relu_of(c + 1, 1 - par, m + AHEAD - NT)
                    if more and m == LAST_TOP + 2:
                        copy_shift(c + 1, 1 - par)
                    exp_of(c, m)
                    if m == 0 and not first:
                        act.wait_ge(pv_done, c * NT)
                        nc.scalar.activation(attended[:], weighted[:], ACT.Copy).then_inc(attended_done, 1)
            over_chunks(chunk)(act)
            act.wait_ge(pv_done, NCH * NT)
            nc.scalar.activation(attended[:], weighted[:], ACT.Copy).then_inc(attended_done, 1)

        @block.vector
        def _(dve):
            chain = chained(dve, norm_chain)
            aggregate(nc, T, range(NT - TPC, NT)).then_inc(stats_done, 1)
            dve.wait_ge(stats_done, 1)
            norm_factors(nc, dve, T, range(NT), 0, chain, sqrt_done, var_ready)
            dve.wait_ge(T["nodes_ready"], 48)

            def centre(k):
                for j in range(TPC):
                    t = k * TPC + j
                    last = nc.vector.tensor_scalar(centred[:, k, j * P:(j + 1) * P], nodes[:, t, :],
                                                   T["moments"][:, t, 0:1], T["rstd"][:, t:t + 1],
                                                   ALU.subtract, ALU.mult)
                last.then_inc(centred_ready[0], 1)
            centre(0)
            centre(2)
            dve.wait_ge(w_turned, 1)
            nc.vector.tensor_copy(w_ht[:], rows[:, 0:P]).then_inc(w_copied, 1)
            dve.wait_ge(w_turned, 2)
            nc.vector.tensor_copy(w_hf[:, D:D + 2], ps_f[:, 0:2]).then_inc(w_copied, 1)
            dve.wait_ge(w_copied, 2)
            nc.vector.tensor_scalar(w_f2all[:], ones[:], w_hf[:, D + 1:D + 2], None,
                                    ALU.mult).then_inc(w_folded, 1)

            def top_waits(c, par, units, first):
                for u in units:
                    if u % WIDES == 0:
                        dve.wait_ge(mask_loaded[par][u // WIDES], mask_loads(c, par))
                if units:
                    need(dve, top_done, c * TPC * WIDES + (first + len(units) - 4))

            def top_of(c, par, u, slot):
                j, g = u // WIDES, u % WIDES
                nc.vector.tensor_tensor_reduce(
                    out=junk[:, slot % 4, :], in0=f2_all[:, g * WIDE:(g + 1) * WIDE],
                    in1=mask[:, 1 - par, j, g * WIDE:(g + 1) * WIDE],
                    scale=1.0, scalar=LOWEST, op0=ALU.add, op1=ALU.max,
                    accum_out=row_max[:, j, g:g + 1]).then_inc(top_done, 1)

            centre(4)
            centre(6)

            def tops_first(g, tiles):
                dve.wait_ge(all_done, (g + 1) * (WIDE // CH))
                for j in tiles:
                    top_waits(0, 0, [j * WIDES + g], g * TPC + j)
                    top_of(0, 0, j * WIDES + g, g * TPC + j)

            for k in range(NCH):
                dve.wait_ge(h_done, k + 1)
                for pair in range(2):
                    tiles = slice(k * TPC + 2 * pair, k * TPC + 2 * pair + 2)
                    last = nc.vector.tensor_copy(f_col[:, tiles, :], ps_hf[k % 2][pair][:, :, D:D + 2])
                last.then_inc(f_done, 1)
                if k > 1:
                    tops_first(k // 2 - 1, range(TPC // 2) if k % 2 == 0 else range(TPC // 2, TPC))
            dve.wait_ge(f_done, NCH)
            nc.vector.tensor_scalar(f2_relu[:], f_col[:, :, 1], 1.0 - SLOPE1, None, ALU.mult).then_inc(f_scaled, 1)
            nc.vector.tensor_scalar(f2_exp[:], f_col[:, :, 1], SLOPE1, None, ALU.mult).then_inc(f_scaled, 1)
            nc.vector.tensor_scalar(f1_slope[:], f_col[:, :, 0], SLOPE1, None, ALU.mult).then_inc(f_scaled, 1)
            dve.wait_ge(f1_turned, 1)
            nc.vector.tensor_copy(f1_rows[:], rows[0:NT, 0:P]).then_inc(f1_ready, 1)
            tops_first(WIDES - 1, range(TPC))
            dve.wait_ge(f_scaled, 3)

            def shift_of(c):
                steps = [0]

                def step(instruction):
                    steps[0] += 1
                    instruction.then_inc(shift_done, 1)
                    dve.wait_ge(shift_done, c * NSH + steps[0])
                f1 = f_col[:, bass.ds(c * TPC, TPC), 0]
                dve.wait_ge(top_done, (c + 1) * TPC * WIDES)
                step(nc.vector.tensor_reduce(tops[:, 0, :], row_max[:], AX.X, ALU.max))
                step(nc.vector.tensor_tensor(tops[:, 1, :], tops[:, 0, :], f1, ALU.add))
                step(nc.vector.scalar_tensor_tensor(tops[:, 2, :], tops[:, 1, :], SLOPE1, tops[:, 1, :],
                                                    ALU.mult, ALU.max))
                step(nc.vector.tensor_tensor(tops[:, 0, :], f1_slope[:, bass.ds(c * TPC, TPC)], tops[:, 2, :],
                                             ALU.subtract))
                step(nc.vector.tensor_copy(shift[:, :, 0], tops[:, 0, :]))
                nc.vector.tensor_tensor(shift[:, :, 1], tops[:, 0, :], shift[:, :, 0].bitcast(F32),
                                        ALU.subtract).then_inc(shift_done, 1)

            shift_of(0)

            def finish(e):
                dve.wait_ge(den_done, e + 1)
                nc.vector.reciprocal(rden[:], misc[:, 0:TPC]).then_inc(epilogue, 1)
                dve.wait_ge(out_turned, e + 1)
                dve.wait_ge(x1_loaded, (e + 1) * 16)
                dve.wait_ge(epilogue, (e + 1) * NEPI + 1)
                for j in range(TPC):
                    cols = slice(j * P, (j + 1) * P)
                    last = nc.vector.scalar_tensor_tensor(result[:, cols], rows[:, cols], rden[:, j:j + 1],
                                                          x1_rows[:, cols],
                                                          ALU.mult, ALU.add)
                last.then_inc(epilogue, 1)

            def chunk(c, par):
                first = isinstance(c, int) and c == 0
                more = not isinstance(c, int) or c + 1 < NCH
                for m in range(NT):
                    if m == 6 and not first:
                        finish(c - 1)
                    tops = tops_at(m) if more else []
                    dve.wait_ge(relu_done, c * NT + (m + 1))
                    dve.wait_ge(scores_done, c * NT + (m + 1))
                    top_waits(c + 1, 1 - par, tops, tops[0] if tops else 0)
                    need(dve, exp_done, c * NT + (m - RING + 1))
                    nc.vector.tensor_tensor(arg[:, m % RING, :], scores[m % RING][:], relu[:, m % RING, :],
                                            ALU.add).then_inc(arg_done, 1)
                    for u in tops:
                        top_of(c + 1, 1 - par, u, u)
                    if more and m == LAST_TOP + 1:
                        shift_of(c + 1)
            over_chunks(chunk)(dve)
            finish(NCH - 1)

        @block.tensor
        def _(pe):
            pe.wait_ge(w_loaded, 32)
            nc.tensor.transpose(rows[:, 0:P], w_hf[:, 0:D], ident[:]).then_inc(w_turned, 1)
            pe.wait_ge(w_copied, 1)
            nc.tensor.matmul(ps_f[:, 0:2], w_ht[:], a_col[:], start=True, stop=True).then_inc(w_turned, 1)
            pe.wait_ge(w_folded, 1)

            def turn(k):
                pe.wait_ge(centred_ready[k % 2], k // 2 + 1)
                need(pe, ht_ready, k - 1)
                for j in range(TPC):
                    cols = slice(j * P, (j + 1) * P)
                    last = nc.tensor.transpose(ps_t[k % 2][:, cols], centred[:, k, cols], ident[:])
                last.then_inc(turned, 1)

            turn(0)
            for k in range(NCH):
                if k + 1 < NCH:
                    turn(k + 1)
                pe.wait_ge(ht_ready, k + 1)
                need(pe, all_done, k - 1)
                nc.tensor.matmul(ps_f2[k % 2][:], w_f2all[:], ht[:, k % 2, :], start=True,
                                 stop=True).then_inc(projected, 1)
                need(pe, h_done, k - 1)
                need(pe, f_done, k - 1)
                for j in range(TPC):
                    last = nc.tensor.matmul(ps_hf[k % 2][j // 2][:, j % 2, :], ht[:, k % 2, j * P:(j + 1) * P],
                                            w_hf[:], start=True, stop=True)
                last.then_inc(projected, 1)

            def turn_shift(c):
                pe.wait_ge(shift_done, (c + 1) * NSH)
                for j in range(TPC):
                    last = nc.tensor.matmul(rows[0:2, j * P:(j + 1) * P], shift[:, j, :], ident_r[:],
                                            start=True, stop=True)
                last.then_inc(shift_turned, 1)

            pe.wait_ge(h_done, NCH)
            pe.wait_ge(f_done, NCH)
            nc.tensor.transpose(rows[0:NT, 0:P], f_col[:, :, 0], ident[:]).then_inc(f1_turned, 1)
            pe.wait_ge(f1_ready, 1)
            turn_shift(0)

            def score(c, par, m):
                bank = scores[m % RING]
                if m == 0:
                    pe.wait_ge(shift_copied, c + 1)
                    for j in range(TPC):
                        pe.wait_ge(mask_loaded[par][j], mask_loads(c, par))
                need(pe, arg_done, c * NT + (m - RING + 1))
                nc.tensor.matmul(bank[:], ones_r[:], shift_row[:, par, :], start=True, stop=False)
                for j in range(TPC):
                    last = nc.tensor.matmul(bank[:, j * P:(j + 1) * P], mask[:, 1 - par, j, m * P:(m + 1) * P],
                                            ident16[:], start=False, stop=(j == TPC - 1))
                last.then_inc(scores_done, 1)

            def weigh(c, m):
                pe.wait_ge(exp_done, c * NT + (m + 1))
                nc.tensor.matmul(weighted[:], values[:, m, :], probs[:, m % RING, :], start=(m == 0),
                                 stop=(m == NT - 1)).then_inc(pv_done, 1)

            def denominators(e):
                pe.wait_ge(sum_done, (e + 1) * NT)
                pe.wait_ge(epilogue, (e + 1) * NEPI)
                for j in range(TPC):
                    last = nc.tensor.matmul(misc[:, j:j + 1], sums[:, j * P:(j + 1) * P], ones[:, 0:1],
                                            start=True, stop=True)
                last.then_inc(den_done, 1)

            def turn_out(e):
                pe.wait_ge(shift_copied, e + 1)
                for j in range(TPC):
                    cols = slice(j * P, (j + 1) * P)
                    last = nc.tensor.transpose(rows[:, cols], attended[:, cols], ident[:])
                last.then_inc(out_turned, 1)

            for m in range(AHEAD):
                score(0, 0, m)

            def chunk(c, par):
                first = isinstance(c, int) and c == 0
                more = not isinstance(c, int) or c + 1 < NCH
                for m in range(NT):
                    if m + AHEAD < NT:
                        score(c, par, m + AHEAD)
                    elif more:
                        score(c + 1, 1 - par, m + AHEAD - NT)
                    if more and m == LAST_TOP + 2:
                        turn_shift(c + 1)
                    if m == 0 and not first:
                        weigh(c - 1, NT - 1)
                    if m == 1 and not first:
                        denominators(c - 1)
                        pe.wait_ge(attended_done, c)
                    if m > 0:
                        weigh(c, m - 1)
                    if m == 2 and not first:
                        turn_out(c - 1)
            over_chunks(chunk)(pe)
            weigh(NCH - 1, NT - 1)
            denominators(NCH - 1)
            pe.wait_ge(attended_done, NCH)
            turn_out(NCH - 1)


def kernel(x, adj, L0_gnn_Wq, L0_gnn_Wk, L0_gnn_Wv, L0_gnn_weightr, L0_gnn_weightd, L0_gnn_bias,
           L1_gnn_weight, L1_gnn_weight_a1, L1_gnn_weight_a2):
    import numpy as np
    import concourse.bacc as bacc
    from concourse.bass_utils import run_bass_kernel_spmd

    arrays = dict(
        x=np.ascontiguousarray(x), adj=np.ascontiguousarray(adj),
        wq=np.ascontiguousarray(L0_gnn_Wq), wk=np.ascontiguousarray(L0_gnn_Wk),
        wv=np.ascontiguousarray(L0_gnn_Wv),
        wo=np.stack([np.asarray(L0_gnn_weightr), np.asarray(L0_gnn_weightd)]),
        bias=np.ascontiguousarray(L0_gnn_bias), w1=np.ascontiguousarray(L1_gnn_weight),
        a12=np.concatenate([np.asarray(L1_gnn_weight_a1), np.asarray(L1_gnn_weight_a2)], axis=1))
    nc = bacc.Bacc("TRN2", target_bir_lowering=False, num_devices=1)
    args = [nc.dram_tensor(n, a.shape, mybir.dt.from_np(a.dtype), kind="ExternalInput").ap()
            for n, a in arrays.items()]
    out = nc.dram_tensor("out", (N, D), F32, kind="ExternalOutput").ap()
    build(nc, *args, out)
    r = run_bass_kernel_spmd(nc, [arrays], core_ids=[0])
    return r.results[0]["out"]
```
